# Optimizing a Trainium2 kernel written in Bass

```python
import numpy as np
import jax
import jax.numpy as jnp

def _softmax(x, axis=-1):
    return jax.nn.softmax(x, axis=axis)

def _gelu(x):
    return jax.nn.gelu(x, approximate=True)

def _silu(x):
    return jax.nn.silu(x)

def _sigmoid(x):
    return jax.nn.sigmoid(x)

def _layernorm(x, axis=-1, eps=1e-05):
    m = jnp.mean(x, axis=axis, keepdims=True)
    v = jnp.var(x, axis=axis, keepdims=True)
    return (x - m) / jnp.sqrt(v + eps)

def _scatter_add(tgt, idx, src, axis=0):
    return tgt.at[idx].add(src)

def _segment_sum(src, seg, n):
    return jax.ops.segment_sum(src, seg, n)
kernel_name = 'mk_xattn_seq_d2_seqx_r2_90470f'

def setup_inputs(seed: int=0):
    np.random.seed(seed)
    _w = jnp.asarray

    def _rec_inputs():
        import jax
        import jax.numpy as jnp
        _rk = jax.random.key(seed)
        x = -0.0003929 + 0.9999 * jax.random.normal(jax.random.fold_in(_rk, 1), (1, 4096, 512), jnp.float32)
        _lenS = 4096 - jax.random.randint(jax.random.fold_in(_rk, 7), (1,), 0, max(1, 4096 // 4) + 1, jnp.int32)
        _lenS2 = 3202 - jax.random.randint(jax.random.fold_in(_rk, 8), (1,), 0, max(1, 3202 // 4) + 1, jnp.int32)
        _ctx_1024P = jax.random.normal(jax.random.fold_in(_rk, 11), (1, 16, 512), jnp.float32)
        _ctx_1024c = jax.random.dirichlet(jax.random.fold_in(_rk, 511), 0.3 * jnp.ones((16,), jnp.float32), (1, 3202))
        _ctx_1024t = jnp.einsum('bsk,bkd->bsd', _ctx_1024c, _ctx_1024P)
        _ctx_1024t = _ctx_1024t * jax.lax.rsqrt(jnp.mean(jnp.square(_ctx_1024t)) + 1e-12) * 0.953939
        ctx_1024 = 2.81802e-05 + 1.00001 * (_ctx_1024t + 0.3 * jax.random.normal(jax.random.fold_in(_rk, 611), (1, 3202, 512), jnp.float32))
        return (x, ctx_1024)
    x, ctx_1024 = _rec_inputs()

    def _L0_xattn_setup():
        import jax, jax.numpy as jnp
        import numpy as np
        B, L, D = (32, 256, 512)
        H, DK, DV = (8, 16, 16)

        def _xavier(key, shape):
            fan_in, fan_out = (shape[0], shape[1])
            std = (2.0 / (fan_in + fan_out)) ** 0.5
            return std * jax.random.normal(key, shape, dtype=jnp.float32)
        key = jax.random.key(seed)
        ks = jax.random.split(key, 11)
        return {'Q': jax.random.normal(ks[0], (B, L, D), jnp.float32), 'K': jax.random.normal(ks[1], (B, L, D), jnp.float32), 'V': jax.random.normal(ks[2], (B, L, D), jnp.float32), 'W_q': _xavier(ks[3], (D, H * DK)), 'W_k': _xavier(ks[4], (D, H * DK)), 'W_v': _xavier(ks[5], (D, H * DV)), 'W_o': _xavier(ks[6], (H * DV, D)), 'w1': _xavier(ks[7], (D, D)), 'b1': jnp.zeros((D,), jnp.float32), 'w2': _xavier(ks[8], (D, D)), 'b2': jnp.zeros((D,), jnp.float32)}
    _L0_xattn_all = _L0_xattn_setup()
    _L0_xattn_in = {k: v for k, v in _L0_xattn_all.items() if k in ('W_q', 'W_k', 'W_v', 'W_o', 'w1', 'b1', 'w2', 'b2')}
    del _L0_xattn_all

    def _L1_xattn_setup():
        import jax, jax.numpy as jnp
        import numpy as np
        D = 512
        H = 16
        HD = D // H
        DFF = 4 * D
        LN_EPS = 1e-05

        def layernorm(x, gamma, beta):
            mu = jnp.mean(x, axis=-1, keepdims=True)
            var = jnp.mean(jnp.square(x - mu), axis=-1, keepdims=True)
            return (x - mu) * jax.lax.rsqrt(var + LN_EPS) * gamma + beta
        key = jax.random.key(seed)
        ks = jax.random.split(key, 10)
        B, Nq, Nk = (2, 1024, 1024)
        s = 0.02
        return {'q_x': jax.random.normal(ks[0], (B, Nq, D), jnp.float32), 'kv_x': jax.random.normal(ks[1], (B, Nk, D), jnp.float32), 'Wq': jax.random.normal(ks[2], (D, D), jnp.float32) * s, 'Wkv': jax.random.normal(ks[3], (2 * D, D), jnp.float32) * s, 'Wo': jax.random.normal(ks[4], (D, D), jnp.float32) * s, 'bo': jnp.zeros((D,), jnp.float32), 'ln_q_g': jnp.ones((D,), jnp.float32), 'ln_q_b': jnp.zeros((D,), jnp.float32), 'ln_kv_g': jnp.ones((D,), jnp.float32), 'ln_kv_b': jnp.zeros((D,), jnp.float32), 'W1': jax.random.normal(ks[5], (DFF, D), jnp.float32) * s, 'b1': jnp.zeros((DFF,), jnp.float32), 'W2': jax.random.normal(ks[6], (D, DFF), jnp.float32) * s, 'b2': jnp.zeros((D,), jnp.float32)}
    _L1_xattn_all = _L1_xattn_setup()
    _L1_xattn_in = {k: v for k, v in _L1_xattn_all.items() if k in ('Wq', 'Wkv', 'Wo', 'bo', 'ln_q_g', 'ln_q_b', 'ln_kv_g', 'ln_kv_b', 'W1', 'b1', 'W2', 'b2')}
    del _L1_xattn_all
    return {'x': x, 'ctx_1024': ctx_1024, 'L0_xattn_W_q': _L0_xattn_in['W_q'], 'L0_xattn_W_k': _L0_xattn_in['W_k'], 'L0_xattn_W_v': _L0_xattn_in['W_v'], 'L0_xattn_W_o': _L0_xattn_in['W_o'], 'L0_xattn_w1': _L0_xattn_in['w1'], 'L0_xattn_b1': _L0_xattn_in['b1'], 'L0_xattn_w2': _L0_xattn_in['w2'], 'L0_xattn_b2': _L0_xattn_in['b2'], 'L1_xattn_Wq': _L1_xattn_in['Wq'], 'L1_xattn_Wkv': _L1_xattn_in['Wkv'], 'L1_xattn_Wo': _L1_xattn_in['Wo'], 'L1_xattn_bo': _L1_xattn_in['bo'], 'L1_xattn_ln_q_g': _L1_xattn_in['ln_q_g'], 'L1_xattn_ln_q_b': _L1_xattn_in['ln_q_b'], 'L1_xattn_ln_kv_g': _L1_xattn_in['ln_kv_g'], 'L1_xattn_ln_kv_b': _L1_xattn_in['ln_kv_b'], 'L1_xattn_W1': _L1_xattn_in['W1'], 'L1_xattn_b1': _L1_xattn_in['b1'], 'L1_xattn_W2': _L1_xattn_in['W2'], 'L1_xattn_b2': _L1_xattn_in['b2']}

def reference(x, ctx_1024, L0_xattn_W_q, L0_xattn_W_k, L0_xattn_W_v, L0_xattn_W_o, L0_xattn_w1, L0_xattn_b1, L0_xattn_w2, L0_xattn_b2, L1_xattn_Wq, L1_xattn_Wkv, L1_xattn_Wo, L1_xattn_bo, L1_xattn_ln_q_g, L1_xattn_ln_q_b, L1_xattn_ln_kv_g, L1_xattn_ln_kv_b, L1_xattn_W1, L1_xattn_b1, L1_xattn_W2, L1_xattn_b2):
    import jax
    import jax.numpy as jnp

    def _L0_xattn_ref(Q, K, V, W_q, W_k, W_v, W_o, w1, b1, w2, b2):
        import jax, jax.numpy as jnp
        import numpy as np
        B, L, D = (32, 256, 512)
        H, DK, DV = (8, 16, 16)

        def _xavier(key, shape):
            fan_in, fan_out = (shape[0], shape[1])
            std = (2.0 / (fan_in + fan_out)) ** 0.5
            return std * jax.random.normal(key, shape, dtype=jnp.float32)
        b, lq, _ = Q.shape
        lk = K.shape[1]
        Qh = (Q @ W_q).reshape(b, lq, H, DK)
        Kh = (K @ W_k).reshape(b, lk, H, DK)
        Vh = (V @ W_v).reshape(b, lk, H, DV)
        scale = 1.0 / jnp.sqrt(jnp.float32(DK))
        scores = jnp.einsum('bqhd,bkhd->bhqk', Qh, Kh) * scale
        attn = jax.nn.softmax(scores, axis=-1)
        ctx = jnp.einsum('bhqk,bkhd->bqhd', attn, Vh).reshape(b, lq, H * DV)
        attn_out = ctx @ W_o
        X = Q + attn_out
        h = jax.nn.relu(X @ w1.T + b1)
        ffn_out = h @ w2.T + b2
        return ffn_out + X

    def _L1_xattn_ref(q_x, kv_x, Wq, Wkv, Wo, bo, ln_q_g, ln_q_b, ln_kv_g, ln_kv_b, W1, b1, W2, b2):
        import jax, jax.numpy as jnp
        import numpy as np
        D = 512
        H = 16
        HD = D // H
        DFF = 4 * D
        LN_EPS = 1e-05

        def layernorm(x, gamma, beta):
            mu = jnp.mean(x, axis=-1, keepdims=True)
            var = jnp.mean(jnp.square(x - mu), axis=-1, keepdims=True)
            return (x - mu) * jax.lax.rsqrt(var + LN_EPS) * gamma + beta
        B, Nq, _ = q_x.shape
        Nk = kv_x.shape[1]
        scale = HD ** (-0.5)
        q = layernorm(q_x, ln_q_g, ln_q_b) @ Wq.T
        kv = layernorm(kv_x, ln_kv_g, ln_kv_b) @ Wkv.T
        q = q.reshape(B, Nq, H, HD).transpose(0, 2, 1, 3)
        kv = kv.reshape(B, Nk, 2, H, HD).transpose(2, 0, 3, 1, 4)
        k, v = (kv[0], kv[1])
        attn = jnp.einsum('bhqd,bhkd->bhqk', q, k) * scale
        attn = jax.nn.softmax(attn, axis=-1)
        out = jnp.einsum('bhqk,bhkd->bhqd', attn, v)
        out = out.transpose(0, 2, 1, 3).reshape(B, Nq, D)
        x = q_x + out @ Wo.T + bo
        h = jax.nn.silu(x @ W1.T + b1)
        x = x + h @ W2.T + b2
        return x
    x = _L0_xattn_ref(x, ctx_1024, ctx_1024, L0_xattn_W_q, L0_xattn_W_k, L0_xattn_W_v, L0_xattn_W_o, L0_xattn_w1, L0_xattn_b1, L0_xattn_w2, L0_xattn_b2)
    x = _L1_xattn_ref(x, ctx_1024, L1_xattn_Wq, L1_xattn_Wkv, L1_xattn_Wo, L1_xattn_bo, L1_xattn_ln_q_g, L1_xattn_ln_q_b, L1_xattn_ln_kv_g, L1_xattn_ln_kv_b, L1_xattn_W1, L1_xattn_b1, L1_xattn_W2, L1_xattn_b2)
    return x

_drawn_inputs = setup_inputs


def setup_inputs(seed=0):
    import zlib

    import numpy as np

    out = dict(_drawn_inputs(seed))
    spreads = {'L0_xattn_b1': (0.0, 0.1),
     'L0_xattn_b2': (0.0, 0.1),
     'L1_xattn_bo': (0.0, 0.1),
     'L1_xattn_ln_q_g': (1.0, 0.6),
     'L1_xattn_ln_q_b': (0.0, 0.8),
     'L1_xattn_ln_kv_g': (1.0, 0.6),
     'L1_xattn_ln_kv_b': (0.0, 0.532),
     'L1_xattn_b1': (0.0, 0.1),
     'L1_xattn_b2': (0.0, 0.1)}
    factors = {'L1_xattn_Wq': 8.0}
    for name, (base, spread) in spreads.items():
        noise = np.random.default_rng([zlib.crc32(name.encode()), seed]).standard_normal(out[name].shape)
        drawn = base * np.exp(spread * noise) if base else spread * noise
        out[name] = jnp.asarray(drawn.astype(out[name].dtype))
    for name, factor in factors.items():
        out[name] = (out[name] * factor).astype(out[name].dtype)
    return out
```

```python
from contextlib import ExitStack, contextmanager

import concourse.bass as bass
from concourse import mybir

F32 = mybir.dt.float32
F32R = mybir.dt.float32r
ALU = mybir.AluOpType
ACT = mybir.ActivationFunctionType
AX = mybir.AxisListType

P = 128
D = 512
KT = D // P
T = 4096
NB = 512
S = 3202
ST = -(-S // P)
SPAD = ST * P
LN_EPS = 1e-5


def f32(ap):
    return ap.bitcast(F32)


@contextmanager
def phase(nc, name):
    with ExitStack() as ctx:
        sems = []

        def sb(n, shape, dt):
            return ctx.enter_context(nc.sbuf_tensor(f"{name}_{n}", shape, dt))

        def ps(n, shape):
            return ctx.enter_context(nc.psum_tensor(f"{name}_{n}", shape, F32))

        def sem(n):
            sems.append(nc.alloc_semaphore(f"{name}_{n}"))
            return sems[-1]

        yield ctx, sb, ps, sem
    nc.clear_and_free_semaphores(sems)
    nc.all_engine_barrier()


class Step:

    def __init__(self, sem, base=0):
        self.sem, self.base, self.k = sem, base, 0

    def inc(self, ins):
        self.k += 1
        ins.then_inc(self.sem, 1)
        return self.k


def split_weights(nc, sem, name, jobs):
    PIECE = 2048
    pieces = []
    for src, hi, lo in jobs:
        for c in range(0, src.shape[1], PIECE):
            e = min(c + PIECE, src.shape[1])
            pieces.append((src[:, c:e], hi[:, c:e], lo[:, c:e], e - c))
    with ExitStack() as inner:
        stage = inner.enter_context(nc.sbuf_tensor(f"{name}_stage", [P, 2, PIECE], F32))
        loaded = [sem(f"w_loaded{i}") for i in range(2)]
        hi_done, lo_done = sem("w_hi_done"), sem("w_lo_done")
        block = inner.enter_context(nc.Block())

        @block.sync
        def _(sp):
            for i, (src, _, _, w) in enumerate(pieces):
                if i >= 2:
                    sp.wait_ge(lo_done, i - 1)
                sp.dma_start(stage[:, i % 2, 0:w], src).then_inc(loaded[i % 2], 16)

        @block.scalar
        def _(act):
            for i, (_, hi, _, w) in enumerate(pieces):
                act.wait_ge(loaded[i % 2], 16 * (i // 2 + 1))
                act.activation(hi, stage[:, i % 2, 0:w], ACT.Copy).then_inc(hi_done, 1)

        @block.vector
        def _(dve):
            for i, (_, hi, lo, w) in enumerate(pieces):
                dve.wait_ge(loaded[i % 2], 16 * (i // 2 + 1))
                dve.wait_ge(hi_done, i + 1)
                dve.tensor_tensor(lo, stage[:, i % 2, 0:w], f32(hi), ALU.subtract).then_inc(lo_done, 1)


def rows(w, width):
    return [w[k * P:(k + 1) * P, 0:width] for k in range(w.shape[0] // P)]


def weight(nc, ctx, name, kt, width):
    hi = ctx.enter_context(nc.sbuf_tensor(f"{name}_hi", [P, kt, width], F32R))
    lo = ctx.enter_context(nc.sbuf_tensor(f"{name}_lo", [P, kt, width], F32R))
    return hi, lo


def weight_jobs(w, dram):
    return [(src, w[0][:, k, :], w[1][:, k, :]) for k, src in enumerate(rows(dram, dram.shape[1]))]


def project(nc, name, x, tokens, weights, outs, ln=None):
    RING = 4
    full, rest = divmod(tokens, NB)
    rest_pad = -(-rest // P) * P
    use_raw = any(o[0] == "raw" for o in outs)

    def products(width):
        found = []
        for src, wname, kind, dst in outs:
            if kind == "rows":
                found += [(src, wname, kind, dst, m) for m in range(dst.shape[1] // P)]
            else:
                found += [(src, wname, kind, dst, t) for t in range(width // P)]
        return found

    R = len(products(NB))
    uses = [len(range(s, R, RING)) for s in range(RING)]

    with phase(nc, name) as (ctx, sb, ps, sem):

        W = {n: weight(nc, ctx, f"{name}_{n}", KT, w.shape[1]) for n, w in weights.items()}
        split_weights(nc, sem, name, [j for n, w in weights.items() for j in weight_jobs(W[n], w)])

        xt = sb("xt", [P, KT, NB], F32)
        xh, xl = sb("xh", [P, KT, NB], F32R), sb("xl", [P, KT, NB], F32R)
        xc = sb("xc", [P, KT, NB], F32)
        sq = sb("sq", [P, KT, NB], F32)
        zh, zl = sb("zh", [P, KT, NB], F32R), sb("zl", [P, KT, NB], F32R)
        sqh, sql = sb("sqh", [P, KT, NB], F32R), sb("sql", [P, KT, NB], F32R)
        std, rstd = sb("std", [P, NB], F32), sb("rstd", [P, NB], F32)
        gb = sb("gb", [P, 2, KT], F32)
        eps = sb("eps", [P, 1], F32)
        inv_d = sb("inv_d", [P, P], F32)
        inv_dr = sb("inv_dr", [P, P], F32R)
        out = [sb(f"out{i}", [P, 1024], F32R) for i in range(RING)]
        prod = [ps(f"prod{i}", [P, NB]) for i in range(RING)]
        mean, var = ps("mean", [P, NB]), ps("var", [P, NB])

        x_loaded, const_loaded, consts_done = sem("x_loaded"), sem("const_loaded"), sem("consts_done")
        dve_steps, act_steps, stats_done = sem("dve_steps"), sem("act_steps"), sem("stats_done")
        prod_done = [sem(f"prod_done{i}") for i in range(RING)]
        hi_done = [sem(f"hi_done{i}") for i in range(RING)]
        lo_done = [sem(f"lo_done{i}") for i in range(RING)]
        stored = [sem(f"stored{i}") for i in range(RING)]
        NDVE = 2 if ln is None else 12
        NACT = 3

        def blocks(eng, body):
            with eng.Fori(0, full) as n:
                body(n, NB, NB)
            if rest:
                body(full, rest, rest_pad)

        def source(which):
            return (xh, xl) if which == "raw" else (zh, zl)

        def halves(s, kind, dst, wp):
            if kind == "rows":
                return out[s][:, 0:wp], out[s][:, NB:NB + wp], prod[s][:, 0:wp]
            H, hd = dst.shape[0], dst.shape[3] // 2
            o = out[s][:, 0:H * 2 * hd].rearrange("p (h d) -> p h d", h=H)
            return o[:, :, 0:hd], o[:, :, hd:2 * hd], prod[s][:, 0:H * hd].rearrange("p (h d) -> p h d", h=H)

        def products_read(eng, n):
            last = (R - 1) % RING
            eng.wait_ge(prod_done[last], n * uses[last])

        block = ctx.enter_context(nc.Block())

        @block.sync
        def _(sp):
            if ln is not None:
                sp.dma_start(gb[:, 0, :], ln[0][:, :]).then_inc(const_loaded, 16)
                sp.dma_start(gb[:, 1, :], ln[1][:, :]).then_inc(const_loaded, 16)

            def body(n, w, wp):
                sp.wait_ge(dve_steps, n * NDVE)
                sp.dma_start(xt[:, :, 0:w], x.rearrange("(k p) t -> p k t", p=P)[:, :, bass.ds(n * NB, w)]).then_inc(x_loaded, 16)
                for i, (src, wn, kind, dst, m) in enumerate(products(wp)):
                    s = i % RING
                    sp.wait_ge(lo_done[s], n * uses[s] + i // RING + 1)
                    if kind == "rows":
                        to = dst[:, m * P:(m + 1) * P, bass.ds(n * NB, wp)].rearrange("s p c -> p s c")
                        of = f32(out[s][:, 0:2 * NB]).rearrange("p (s c) -> p s c", s=2)[:, :, 0:wp]
                    else:
                        H, hd2 = dst.shape[0], dst.shape[3]
                        to = dst[:, :, bass.ds(n * (NB // P) + m, 1), :].rearrange("h p t d -> p h (t d)")
                        of = f32(out[s][:, 0:H * hd2]).rearrange("p (h d) -> p h d", h=H)
                    sp.dma_start(to, of).then_inc(stored[s], 16)

            blocks(sp, body)
            tail = products(rest_pad) if rest else []
            for s in range(RING):
                count = full * uses[s] + len(range(s, len(tail), RING))
                if count:
                    sp.wait_ge(stored[s], 16 * count)

        @block.scalar
        def _(act):
            if ln is not None:
                act.wait_ge(consts_done, 3)

            def body(n, w, wp):
                if ln is not None:
                    act.wait_ge(dve_steps, n * NDVE + 3)
                    act.wait_ge(stats_done, n * 2)
                    act.activation(sq[:, :, 0:w], xc[:, :, 0:w], ACT.Square).then_inc(act_steps, 1)
                    act.wait_ge(act_steps, n * NACT + 1)
                    act.activation(sqh[:, :, 0:w], sq[:, :, 0:w], ACT.Copy).then_inc(act_steps, 1)
                    act.wait_ge(stats_done, n * 2 + 2)
                    act.activation(std[:, 0:w], var[:, 0:w], ACT.Sqrt, bias=eps[:, 0:1]).then_inc(act_steps, 1)
                for i, (src, wn, kind, dst, m) in enumerate(products(wp)):
                    s = i % RING
                    act.wait_ge(prod_done[s], n * uses[s] + i // RING + 1)
                    act.wait_ge(stored[s], (n * uses[s] + i // RING) * 16)
                    hi, _, y = halves(s, kind, dst, wp)
                    act.activation(hi, y, ACT.Copy).then_inc(hi_done[s], 1)

            blocks(act, body)

        @block.vector
        def _(dve):
            if ln is not None:
                dve.memset(eps[:], LN_EPS).then_inc(consts_done, 1)
                dve.memset(inv_d[:], 1.0 / D).then_inc(consts_done, 1)
                dve.wait_ge(consts_done, 2)
                dve.tensor_copy(inv_dr[:], inv_d[:]).then_inc(consts_done, 1)
                dve.wait_ge(const_loaded, 32)

            def body(n, w, wp):
                step = Step(dve_steps, n * NDVE)

                def chain(ins):
                    step.inc(ins)
                    dve.wait_ge(dve_steps, n * NDVE + step.k)

                if wp > w:
                    for t in (xh, xl) + ((zh, zl) if ln is not None else ()):
                        products_read(dve, n)
                        dve.memset(f32(t[:, :, w:wp]), 0.0)
                dve.wait_ge(x_loaded, n * 16 + 16)
                products_read(dve, n)
                chain(dve.tensor_copy(xh[:, :, 0:w], xt[:, :, 0:w]))
                chain(dve.tensor_tensor(xl[:, :, 0:w], xt[:, :, 0:w], f32(xh[:, :, 0:w]), ALU.subtract))
                if ln is not None:
                    wide = [P, KT, w]
                    dve.wait_ge(stats_done, n * 2 + 1)
                    chain(dve.tensor_tensor(xc[:, :, 0:w], xt[:, :, 0:w],
                                            mean[:, 0:w].unsqueeze(1).to_broadcast(wide), ALU.subtract))
                    dve.wait_ge(act_steps, n * NACT + 2)
                    chain(dve.tensor_tensor(sql[:, :, 0:w], sq[:, :, 0:w], f32(sqh[:, :, 0:w]), ALU.subtract))
                    dve.wait_ge(act_steps, n * NACT + 3)
                    chain(dve.reciprocal(rstd[:, 0:w], std[:, 0:w]))
                    chain(dve.tensor_tensor(sq[:, :, 0:w], xc[:, :, 0:w],
                                            rstd[:, 0:w].unsqueeze(1).to_broadcast(wide), ALU.mult))
                    for k in range(KT):
                        last = dve.tensor_scalar(xc[:, k, 0:w], sq[:, k, 0:w], gb[:, 0, k:k + 1], gb[:, 1, k:k + 1],
                                                 ALU.mult, ALU.add)
                        step.inc(last)
                    dve.wait_ge(dve_steps, n * NDVE + step.k)
                    chain(dve.tensor_copy(zh[:, :, 0:w], xc[:, :, 0:w]))
                    chain(dve.tensor_tensor(zl[:, :, 0:w], xc[:, :, 0:w], f32(zh[:, :, 0:w]), ALU.subtract))
                assert step.k == NDVE
                for i, (src, wn, kind, dst, m) in enumerate(products(wp)):
                    s = i % RING
                    dve.wait_ge(hi_done[s], n * uses[s] + i // RING + 1)
                    hi, lo, y = halves(s, kind, dst, wp)
                    dve.tensor_tensor(lo, y, f32(hi), ALU.subtract).then_inc(lo_done[s], 1)

            blocks(dve, body)

        @block.tensor
        def _(pe):
            if ln is not None:
                pe.wait_ge(consts_done, 3)

            def body(n, w, wp):
                pe.wait_ge(dve_steps, n * NDVE + 2)
                if ln is not None:
                    for stat, (h, l), need in ((mean, (xh, xl), 2), (var, (sqh, sql), 4)):
                        pe.wait_ge(dve_steps, n * NDVE + need)
                        for i in range(2 * KT):
                            mm = pe.matmul(stat[:, 0:w], inv_dr[:], (h, l)[i // KT][:, i % KT, 0:w],
                                           start=(i == 0), stop=(i == 2 * KT - 1))
                        mm.then_inc(stats_done, 1)
                    pe.wait_ge(dve_steps, n * NDVE + 12)
                for i, (src, wn, kind, dst, m) in enumerate(products(wp)):
                    s = i % RING
                    pe.wait_ge(lo_done[s], n * uses[s] + i // RING)
                    xs, ws = source(src), W[wn]
                    terms = [(k, a, b) for k in range(KT) for a, b in ((0, 0), (0, 1), (1, 0))]
                    for j, (k, a, b) in enumerate(terms):
                        if kind == "rows":
                            o, l, r = prod[s][:, 0:wp], ws[a][:, k, m * P:(m + 1) * P], xs[b][:, k, 0:wp]
                        else:
                            c = ws[a].shape[2]
                            o, l, r = prod[s][:, 0:c], xs[b][:, k, m * P:(m + 1) * P], ws[a][:, k, :]
                        mm = pe.matmul(o, l, r, start=(j == 0), stop=(j == len(terms) - 1))
                    mm.then_inc(prod_done[s], 1)

            blocks(pe, body)



GROUPS = ST // 2
RINGS = [0, 1, 2, 3] * (GROUPS // 4) + [4]
LAG = 3
CHUNKS = 3
CHUNK = -(-S // CHUNKS) // 2 * 2 + 2 * (-(-S // CHUNKS) % 2)
UNITS = (NB // P) * CHUNKS
UNITS_AT = {1: [0], 2: [1], 3: [2], 4: [3], 5: [4, 5], 6: [6], 7: [7], 8: [8], 9: [9], 10: [10, 11]}
ROW_AT = 12
POOL_LO = (1, 4, 7, 10)
DVE_HI = (3, 9)
QB = T // NB


class Item:

    def __init__(self, pair, k, qb, j, half, prev_k=None, next_k=None, first=False, last=False, final_head=False):
        self.final_head = final_head
        self.pair, self.k, self.qb, self.j = pair, k, qb, j
        self.h = pair * 2 + k
        self.n = self.h * QB + qb
        self.use = self.h * (QB // 2) + half
        self.prev_use = self.use if j == 1 else self.use - 1
        self.next_use = self.use if j == 0 else self.use + 1
        self.prev_k = k if prev_k is None else prev_k
        self.next_k = k if next_k is None else next_k
        self.starts_head, self.ends_head = prev_k is not None, next_k is not None
        self.first, self.last = first, last


def attention(nc, name, H, hd, q, k, v, acc_out):
    SCALE = float(hd) ** -0.5
    ROW = -(-3 * hd // 32) * 32
    C = ROW + 1
    M = 96
    PAIRS = H // 2
    LAST_KEYS = S - (ST - 1) * P

    with phase(nc, name) as (ctx, sb, ps, sem):

        kt = [sb(f"k{i}", [C, SPAD], F32R) for i in range(2)]
        vt = [sb(f"v{i}", [P, ST, M], F32R) for i in range(2)]
        qt = [sb(f"q{i}", [C, NB], F32R) for i in range(2)]
        prob = [sb(f"prob{i}", [P, 2 * NB], F32) for i in range(5)]
        phi = [sb(f"phi{i}", [P, 2 * NB], F32R) for i in range(5)]
        plo = [sb(f"plo{i}", [P, 2 * NB], F32R) for i in range(5)]
        acc_sb = [sb(f"acc_sb{i}", [M, NB], F32) for i in range(2)]
        maxes = sb("maxes", [P, NB // P, CHUNKS], F32)
        negmax = sb("negmax", [P, NB // P], F32)
        ident = sb("ident", [P, P], F32)

        score = [ps(f"score{i}", [P, 2 * NB]) for i in range(2)]
        mscore = ps("mscore", [P, 3 * NB])
        acc = ps("acc", [M, NB])

        k_loaded = [sem(f"k_loaded{i}") for i in range(2)]
        v_loaded = [sem(f"v_loaded{i}") for i in range(2)]
        q_loaded = [sem(f"q_loaded{i}") for i in range(2)]
        filled, ident_done = sem("filled"), sem("ident_done")
        score_done = [sem(f"score_done{i}") for i in range(2)]
        exp_done = [sem(f"exp_done{i}") for i in range(5)]
        hi_done = [sem(f"hi_done{i}") for i in range(5)]
        lo_done = [sem(f"lo_done{i}") for i in range(5)]
        pv_done = [sem(f"pv_done{i}") for i in range(5)]
        unit_done, unit_read = sem("unit_done"), sem("unit_read")
        neg_done, row_done, row_copied = sem("neg_done"), sem("row_done"), sem("row_copied")
        acc_copied = sem("acc_copied")
        acc_stored = [sem(f"acc_stored{i}") for i in range(2)]

        def items(eng):
            def pair(p, first, last):
                for kk in range(2):
                    yield Item(p, kk, 0, 0, 0, prev_k=1 - kk, first=first and kk == 0,
                               final_head=last and kk == 1)
                    with eng.Fori(0, QB // 2 - 1) as i:
                        yield Item(p, kk, i * 2 + 1, 1, i)
                        yield Item(p, kk, i * 2 + 2, 0, i + 1)
                    yield Item(p, kk, QB - 1, 1, QB // 2 - 1, next_k=1 - kk, last=last and kk == 1)

            yield from pair(0, True, False)
            with eng.Fori(1, PAIRS - 1) as p:
                yield from pair(p, False, False)
            yield from pair(PAIRS - 1, False, True)

        def steps(it):
            return range(GROUPS + LAG) if it.last else range(GROUPS)

        def ring_uses(it, g):
            return it.n * RINGS.count(RINGS[g]) + RINGS[:g].count(RINGS[g])

        def score_buffer(j, use, g):
            x = j * GROUPS + g
            return x % 2, use * GROUPS + x // 2

        def lagged(it, s, lag):
            g = s - lag
            if g >= GROUPS or (g < 0 and it.first):
                return None
            if g >= 0:
                return g, RINGS[g], ring_uses(it, g), it.k
            g += GROUPS
            r = RINGS[g]
            return g, r, it.n * RINGS.count(r) - RINGS[g:].count(r), it.prev_k

        FILLS, REFILLS = [], []
        for i in range(2):
            FILLS.append((f32(vt[i][:]), 1.0))
            REFILLS.append((f32(vt[i][:, ST - 1, 2 * hd:M]), 0.0))
            FILLS += [(f32(kt[i][ROW:C, 0:S]), 1.0), (f32(kt[i][ROW:C, S:SPAD]), 0.0)]
            if ROW > 3 * hd:
                FILLS += [(f32(kt[i][ROW - 32:ROW, :]), 0.0), (f32(qt[i][ROW - 32:ROW, :]), 0.0)]
        TOP = [(f32(vt[i][0:LAST_KEYS, ST - 1, 2 * hd:M]), 1.0) for i in range(2)]
        NFILL = len(FILLS) + len(REFILLS) + len(TOP)

        block = ctx.enter_context(nc.Block())

        @block.sync
        def _(sp):
            def load_kv(h, kk):
                rows = bass.ds(h * hd, hd)
                for at, half in ((0, 0), (hd, 1), (2 * hd, 0)):
                    sp.dma_start(f32(kt[kk][at:at + hd, :]), k[half, rows, :]).then_inc(k_loaded[kk], 16)
                sp.dma_start(f32(vt[kk][:, :, 0:2 * hd]),
                             v[bass.ds(h, 1)].rearrange("o p t d -> p (o t) d")).then_inc(v_loaded[kk], 16)

            def load_q(h, qb, j):
                rows, cols = bass.ds(h * hd, hd), bass.ds(qb * NB, NB)
                for at, half in ((0, 0), (hd, 0), (2 * hd, 1)):
                    sp.dma_start(f32(qt[j][at:at + hd, :]), q[half, rows, cols]).then_inc(q_loaded[j], 16)

            def store(h, qb, j, n):
                sp.wait_ge(acc_copied, n + 1)
                sp.dma_start(acc_out[bass.ds(h, 1), :, bass.ds(qb * NB, NB)].rearrange("o r c -> (o r) c"),
                             acc_sb[j][0:3 * hd, :]).then_inc(acc_stored[j], 16)

            sp.wait_ge(filled, NFILL)
            load_kv(0, 0)
            load_q(0, 0, 0)
            for it in items(sp):
                if not it.last:
                    if not it.first:
                        b, before = score_buffer(1 - it.j, it.prev_use, GROUPS - 1)
                        sp.wait_ge(score_done[b], before + 1)
                    if it.ends_head:
                        load_q(it.h + 1, 0, 1 - it.j)
                    else:
                        load_q(it.h, it.qb + 1, 1 - it.j)
                if not it.first:
                    if it.starts_head:
                        store(it.h - 1, QB - 1, 1 - it.j, it.n - 1)
                    else:
                        store(it.h, it.qb - 1, 1 - it.j, it.n - 1)
                if it.starts_head and not it.final_head:
                    if not it.first:
                        sp.wait_ge(pv_done[4], it.h * QB)
                    load_kv(it.h + 1, 1 - it.k)
                if it.last:
                    store(it.h, it.qb, it.j, it.n)
            for j in range(2):
                sp.wait_ge(acc_stored[j], H * (QB // 2) * 16)

        @block.gpsimd
        def _(pool):
            pool.memset(ident[:], 0.0).then_inc(ident_done, 1)
            pool.wait_ge(ident_done, 1)
            pool.affine_select(out=ident[:], in_=ident[:], compare_op=ALU.not_equal, fill=1.0, base=0,
                               pattern=[[-1, P]], channel_multiplier=1).then_inc(ident_done, 1)
            for it in items(pool):
                for s in steps(it):
                    if (x := lagged(it, s, 2)) and x[0] in POOL_LO:
                        _, r, uses, _ = x
                        pool.wait_ge(hi_done[r], uses + 1)
                        pool.tensor_tensor(plo[r][:], prob[r][:], f32(phi[r][:]), ALU.subtract).then_inc(lo_done[r], 1)

        @block.scalar
        def _(act):
            def copy_row(j, n):
                act.wait_ge(row_done, n + 1)
                act.activation(qt[j][ROW:C, :], mscore[0:1, 0:NB], ACT.Copy).then_inc(row_copied, 1)

            def copy_acc(n, j, use):
                act.wait_ge(pv_done[4], n + 1)
                act.wait_ge(acc_stored[j], use * 16)
                act.activation(acc_sb[j][0:3 * hd, :], acc[0:3 * hd, :], ACT.Copy).then_inc(acc_copied, 1)

            copy_row(0, 0)
            for it in items(act):
                for s in steps(it):
                    if s < GROUPS:
                        b, before = score_buffer(it.j, it.use, s)
                        r = RINGS[s]
                        act.wait_ge(score_done[b], before + 1)
                        act.wait_ge(pv_done[r], ring_uses(it, s))
                        act.activation(prob[r][:], score[b][:], ACT.Exp, scale=SCALE).then_inc(exp_done[r], 1)
                    if s == ROW_AT and not it.last:
                        copy_row(1 - it.j, it.n + 1)
                    if (x := lagged(it, s, 1)) and x[0] not in DVE_HI:
                        _, r, uses, _ = x
                        act.wait_ge(exp_done[r], uses + 1)
                        act.activation(phi[r][:], prob[r][:], ACT.Copy).then_inc(hi_done[r], 1)
                    if s == LAG - 1 and not it.first:
                        copy_acc(it.n - 1, 1 - it.j, it.prev_use)
                    if s == GROUPS + LAG - 1:
                        copy_acc(it.n, it.j, it.use)

        @block.vector
        def _(dve):
            def maximum(n, u):
                t, c = divmod(u, CHUNKS)
                w = min(CHUNK, S - c * CHUNK)
                dve.wait_ge(unit_done, n * UNITS + u + 1)
                dve.tensor_reduce(maxes[:, t, c:c + 1], mscore[:, 0:w], AX.X, ALU.max).then_inc(unit_read, 1)
                if u == UNITS - 1:
                    dve.wait_ge(unit_read, n * UNITS + UNITS)
                    dve.tensor_reduce(negmax[:], maxes[:], AX.X, ALU.max, negate=True).then_inc(neg_done, 1)

            for ap, value in FILLS:
                dve.memset(ap, value).then_inc(filled, 1)
            dve.wait_ge(filled, len(FILLS))
            for ap, value in REFILLS:
                dve.memset(ap, value).then_inc(filled, 1)
            dve.wait_ge(filled, len(FILLS) + len(REFILLS))
            for ap, value in TOP:
                dve.memset(ap, value).then_inc(filled, 1)
            for u in range(UNITS):
                maximum(0, u)
            for it in items(dve):
                for s in steps(it):
                    if not it.last:
                        for u in UNITS_AT.get(s, ()):
                            maximum(it.n + 1, u)
                    if (x := lagged(it, s, 1)) and x[0] in DVE_HI:
                        _, r, uses, _ = x
                        dve.wait_ge(exp_done[r], uses + 1)
                        dve.tensor_copy(phi[r][:], prob[r][:]).then_inc(hi_done[r], 1)
                    if (x := lagged(it, s, 2)) and x[0] not in POOL_LO:
                        _, r, uses, _ = x
                        dve.wait_ge(hi_done[r], uses + 1)
                        dve.tensor_tensor(plo[r][:], prob[r][:], f32(phi[r][:]), ALU.subtract).then_inc(lo_done[r], 1)

        @block.tensor
        def _(pe):
            def unit(n, j, kk, u):
                t, c = divmod(u, CHUNKS)
                lo, hi = c * CHUNK, min((c + 1) * CHUNK, S)
                pe.wait_ge(unit_read, n * UNITS + u)
                for at in range(lo, hi, NB):
                    e = min(at + NB, hi)
                    mm = pe.matmul(mscore[:, at - lo:e - lo], qt[j][0:3 * hd, t * P:(t + 1) * P],
                                   kt[kk][0:3 * hd, at:e], start=True, stop=True)
                mm.then_inc(unit_done, 1)

            def make_row(n):
                pe.wait_ge(neg_done, n + 1)
                for t in range(NB // P):
                    mm = pe.matmul(mscore[0:1, t * P:(t + 1) * P], negmax[:, t:t + 1], ident[:], start=True, stop=True)
                mm.then_inc(row_done, 1)

            pe.wait_ge(ident_done, 2)
            pe.wait_ge(k_loaded[0], 48)
            pe.wait_ge(q_loaded[0], 48)
            for u in range(UNITS):
                unit(0, 0, 0, u)
            make_row(0)
            for it in items(pe):
                for s in steps(it):
                    if s < GROUPS:
                        if s == 0:
                            pe.wait_ge(row_copied, it.n + 1)
                        if x := lagged(it, s, 2):
                            pe.wait_ge(exp_done[x[1]], x[2] + 1)
                        b, _ = score_buffer(it.j, it.use, s)
                        for i in range(2):
                            t = 2 * s + i
                            mm = pe.matmul(score[b][:, i * NB:(i + 1) * NB], kt[it.k][:, t * P:(t + 1) * P],
                                           qt[it.j][:], start=True, stop=True)
                        mm.then_inc(score_done[b], 1)
                    if not it.last:
                        if s == 1:
                            pe.wait_ge(q_loaded[1 - it.j], (it.next_use + 1) * 48)
                            if it.ends_head:
                                pe.wait_ge(k_loaded[it.next_k], (it.pair + it.k + 1) * 48)
                        for u in UNITS_AT.get(s, ()):
                            unit(it.n + 1, 1 - it.j, it.next_k, u)
                        if s == ROW_AT:
                            make_row(it.n + 1)
                    if x := lagged(it, s, LAG):
                        g, r, uses, kk = x
                        if g == 0:
                            if it.starts_head:
                                pe.wait_ge(v_loaded[it.k], (it.pair + 1) * 16)
                            pe.wait_ge(acc_copied, it.n)
                        pe.wait_ge(hi_done[r], uses + 1)
                        pe.wait_ge(lo_done[r], uses + 1)
                        for i in range(2):
                            for part in (phi, plo):
                                t = 2 * g + i
                                mm = pe.matmul(acc[:], vt[kk][:, t, :], part[r][:, i * NB:(i + 1) * NB],
                                               start=(t == 0 and part is phi), stop=(t == ST - 1 and part is plo))
                        mm.then_inc(pv_done[r], 1)



def tail(nc, name, H, hd, acc, x, wo, bo, w1, b1, func, w2, b2, out):
    KO = H * hd // P
    HT = P // hd
    F = w1.shape[1]
    FT = F // P

    with phase(nc, name) as (ctx, sb, ps, sem):

        WO, W1, W2 = weight(nc, ctx, f"{name}_wo", KO, D), weight(nc, ctx, f"{name}_w1", KT, F), weight(nc, ctx, f"{name}_w2", FT, D)
        split_weights(nc, sem, name, weight_jobs(WO, wo) + weight_jobs(W1, w1) + weight_jobs(W2, w2))

        bias1 = sb("bias1", [P, FT], F32)
        bias2 = sb("bias2", [P, KT], F32)
        biaso = sb("biaso", [P, KT], F32)
        part = sb("part", [P, 3, KO, NB], F32)
        X = sb("X", [P, KT, NB], F32)
        y = sb("y", [P, KT, NB], F32) if KO < KT else part[:, 1]
        xh, xl = sb("xh", [P, KT, NB], F32R), sb("xl", [P, KT, NB], F32R)
        h = [sb(f"h{i}", [P, NB], F32) for i in range(2)]
        hh = [sb(f"hh{i}", [P, NB], F32R) for i in range(2)]
        hl = [sb(f"hl{i}", [P, NB], F32R) for i in range(2)]
        hp = [ps(f"hp{i}", [P, NB]) for i in range(2)]
        yp = [ps(f"yp{m}", [P, NB]) for m in range(KT)]

        const_loaded, loaded, stored = sem("const_loaded"), sem("acts_loaded"), sem("stored")
        dve_steps = sem("dve_steps")
        wo_done = sem("wo_done")
        hp_done = [sem(f"hp_done{i}") for i in range(2)]
        act_done = [sem(f"act_done{i}") for i in range(2)]
        hh_done = [sem(f"hh_done{i}") for i in range(2)]
        hl_done = [sem(f"hl_done{i}") for i in range(2)]
        used = [sem(f"used{i}") for i in range(2)]
        NCONST = 48 if bo is not None else 32
        NLOAD = 3 * H + 1
        O_LO, X_DONE, X_LO, NDVE = 5, 5 + KT, 7 + KT, 7 + 2 * KT
        HALF = FT // 2
        block = ctx.enter_context(nc.Block())

        @block.sync
        def _(sp):
            sp.dma_start(bias1[:], b1[:, :]).then_inc(const_loaded, 16)
            sp.dma_start(bias2[:], b2[:, :]).then_inc(const_loaded, 16)
            if bo is not None:
                sp.dma_start(biaso[:], bo[:, :]).then_inc(const_loaded, 16)
            with sp.Fori(0, T // NB) as n:
                cols = bass.ds(n * NB, NB)
                sp.wait_ge(stored, n * 16)
                for i in range(3):
                    for hx in range(H):
                        at = hx % HT * hd
                        sp.dma_start(part[at:at + hd, i, hx // HT, :], acc[hx, i * hd:(i + 1) * hd, cols]).then_inc(loaded, 16)
                sp.dma_start(X[:], x.rearrange("(k p) t -> p k t", p=P)[:, :, cols]).then_inc(loaded, 16)
                sp.wait_ge(dve_steps, n * NDVE + NDVE)
                sp.dma_start(out.rearrange("(k p) t -> p k t", p=P)[:, :, cols], y[:]).then_inc(stored, 16)
            sp.wait_ge(stored, T // NB * 16)

        @block.vector
        def _(dve):
            dve.wait_ge(const_loaded, NCONST)
            with dve.Fori(0, T // NB) as n:
                base = n * NDVE
                step = Step(dve_steps)

                def chain(ins):
                    step.inc(ins)
                    dve.wait_ge(dve_steps, base + step.k)

                dve.wait_ge(loaded, n * (NLOAD * 16) + NLOAD * 16)
                chain(dve.tensor_tensor(part[:, 0], part[:, 0], part[:, 1], ALU.add))
                chain(dve.reciprocal(part[:, 2], part[:, 2]))
                chain(dve.tensor_tensor(part[:, 0], part[:, 0], part[:, 2], ALU.mult))
                dve.wait_ge(hp_done[1], n * HALF)
                chain(dve.tensor_copy(xh[:, 0:KO], part[:, 0]))
                chain(dve.tensor_tensor(xl[:, 0:KO], part[:, 0], f32(xh[:, 0:KO]), ALU.subtract))
                dve.wait_ge(wo_done, n + 1)
                for m in range(KT):
                    if bo is not None:
                        step.inc(dve.scalar_tensor_tensor(X[:, m], yp[m][:], biaso[:, m:m + 1], X[:, m], ALU.add, ALU.add))
                    else:
                        step.inc(dve.tensor_tensor(X[:, m], yp[m][:], X[:, m], ALU.add))
                dve.wait_ge(dve_steps, base + step.k)
                chain(dve.tensor_copy(xh[:], X[:]))
                chain(dve.tensor_tensor(xl[:], X[:], f32(xh[:]), ALU.subtract))
                for m in range(FT):
                    b, before = m % 2, n * HALF + m // 2
                    dve.wait_ge(hh_done[b], before + 1)
                    dve.wait_ge(used[b], before)
                    dve.tensor_tensor(hl[b][:], h[b][:], f32(hh[b][:]), ALU.subtract).then_inc(hl_done[b], 1)
                dve.wait_ge(used[1], n * HALF + HALF)
                for m in range(KT):
                    step.inc(dve.scalar_tensor_tensor(y[:, m], yp[m][:], bias2[:, m:m + 1], X[:, m], ALU.add, ALU.add))
                assert step.k == NDVE

        @block.scalar
        def _(act):
            act.wait_ge(const_loaded, NCONST)
            with act.Fori(0, T // NB) as n:
                for m in range(FT):
                    b, before = m % 2, n * HALF + m // 2
                    act.wait_ge(hp_done[b], before + 1)
                    act.wait_ge(hl_done[b], before)
                    act.activation(h[b][:], hp[b][:], func, bias=bias1[:, m:m + 1]).then_inc(act_done[b], 1)
                    act.wait_ge(act_done[b], before + 1)
                    act.wait_ge(used[b], before)
                    act.activation(hh[b][:], h[b][:], ACT.Copy).then_inc(hh_done[b], 1)

        @block.tensor
        def _(pe):
            TERMS = ((0, 0), (0, 1), (1, 0))

            def use_hidden(n, m):
                b, before = m % 2, n * HALF + m // 2
                pe.wait_ge(hl_done[b], before + 1)
                for a, c in TERMS:
                    for d in range(KT):
                        mm = pe.matmul(yp[d][:], W2[a][:, m, d * P:(d + 1) * P], (hh, hl)[c][b][:],
                                       start=(m == 0 and (a, c) == (0, 0)), stop=(m == FT - 1 and (a, c) == (1, 0)))
                mm.then_inc(used[b], 1)

            with pe.Fori(0, T // NB) as n:
                pe.wait_ge(dve_steps, n * NDVE + O_LO)
                for d in range(KT):
                    for i, (k, a, c) in enumerate([(k, a, c) for k in range(KO) for a, c in TERMS]):
                        mm = pe.matmul(yp[d][:], WO[a][:, k, d * P:(d + 1) * P], (xh, xl)[c][:, k],
                                       start=(i == 0), stop=(i == 3 * KO - 1))
                mm.then_inc(wo_done, 1)
                pe.wait_ge(dve_steps, n * NDVE + X_LO)
                for m in range(FT):
                    b, before = m % 2, n * HALF + m // 2
                    pe.wait_ge(act_done[b], before)
                    for i, (k, a, c) in enumerate([(k, a, c) for k in range(KT) for a, c in TERMS]):
                        mm = pe.matmul(hp[b][:], W1[a][:, k, m * P:(m + 1) * P], (xh, xl)[c][:, k],
                                       start=(i == 0), stop=(i == 3 * KT - 1))
                    mm.then_inc(hp_done[b], 1)
                    if m:
                        use_hidden(n, m - 1)
                use_hidden(n, FT - 1)


def build(nc, a, out):
    L0, L1 = (8, 16), (16, 32)

    def scratch(n, shape):
        return nc.dram_tensor(n, shape, F32).ap()

    q, k, v, acc = [], [], [], []
    for i, (H, hd) in enumerate((L0, L1)):
        q.append(scratch(f"q{i}", [2, H * hd, T]))
        k.append(scratch(f"k{i}", [2, H * hd, SPAD]))
        v.append(scratch(f"v{i}", [H, P, ST, 2 * hd]))
        acc.append(scratch(f"acc{i}", [H, 3 * hd, T]))
    x1 = scratch("x1", [D, T])
    ctx_t, x = a["ctx_1024"], a["x"]

    project(nc, "kv", ctx_t, S,
            {"k0": a["L0_xattn_W_k"], "v0": a["L0_xattn_W_v"], "k1": a["L1_xattn_Wkv"][:, 0:D], "v1": a["L1_xattn_Wkv"][:, D:2 * D]},
            [("raw", "k0", "rows", k[0]), ("raw", "v0", "heads", v[0]),
             ("ln", "k1", "rows", k[1]), ("ln", "v1", "heads", v[1])],
            ln=(a["L1_xattn_ln_kv_g"], a["L1_xattn_ln_kv_b"]))
    project(nc, "pq0", x, T, {"q0": a["L0_xattn_W_q"]}, [("raw", "q0", "rows", q[0])])
    attention(nc, "a0", *L0, q[0], k[0], v[0], acc[0])
    tail(nc, "t0", *L0, acc[0], x, a["L0_xattn_W_o"], None, a["L0_xattn_w1"], a["L0_xattn_b1"], ACT.Relu,
         a["L0_xattn_w2"], a["L0_xattn_b2"], x1)
    project(nc, "pq1", x1, T, {"q1": a["L1_xattn_Wq"]}, [("ln", "q1", "rows", q[1])],
            ln=(a["L1_xattn_ln_q_g"], a["L1_xattn_ln_q_b"]))
    attention(nc, "a1", *L1, q[1], k[1], v[1], acc[1])
    tail(nc, "t1", *L1, acc[1], x1, a["L1_xattn_Wo"], a["L1_xattn_bo"], a["L1_xattn_W1"], a["L1_xattn_b1"], ACT.Silu,
         a["L1_xattn_W2"], a["L1_xattn_b2"], out)


TRANSPOSED = {"x", "ctx_1024", "L0_xattn_w1", "L0_xattn_w2", "L1_xattn_Wq", "L1_xattn_Wkv", "L1_xattn_Wo",
              "L1_xattn_W1", "L1_xattn_W2"}


def kernel(**inputs):
    import numpy as np
    import concourse.bacc as bacc
    from concourse.bass_utils import run_bass_kernel_spmd

    nc = bacc.Bacc("TRN2", target_bir_lowering=False, num_devices=1)
    arrays, aps = {}, {}
    for name, value in inputs.items():
        a = np.asarray(value)
        if name in ("x", "ctx_1024"):
            a = a[0]
        if a.ndim == 1:
            a = a.reshape(-1, P)
        if name in TRANSPOSED or value.ndim == 1:
            a = a.T
        a = np.ascontiguousarray(a)
        arrays[f"in_{name}"] = a
        aps[name] = nc.dram_tensor(f"in_{name}", a.shape, mybir.dt.from_np(a.dtype), kind="ExternalInput").ap()
    out = nc.dram_tensor("out_t", (D, T), F32, kind="ExternalOutput").ap()
    build(nc, aps, out)
    r = run_bass_kernel_spmd(nc, [arrays], core_ids=[0])
    return np.ascontiguousarray(r.results[0]["out_t"].T)[None]
```

```python
from contextlib import ExitStack, contextmanager

import concourse.bass as bass
from concourse import mybir

F32 = mybir.dt.float32
F32R = mybir.dt.float32r
ALU = mybir.AluOpType
ACT = mybir.ActivationFunctionType
AX = mybir.AxisListType

P = 128
D = 512
KT = D // P
T = 4096
NB = 512
S = 3202
ST = -(-S // P)
SPAD = ST * P
LN_EPS = 1e-5


def f32(ap):
    return ap.bitcast(F32)


@contextmanager
def phase(nc, name):
    with ExitStack() as ctx:
        sems = []

        def sb(n, shape, dt):
            return ctx.enter_context(nc.sbuf_tensor(f"{name}_{n}", shape, dt))

        def ps(n, shape):
            return ctx.enter_context(nc.psum_tensor(f"{name}_{n}", shape, F32))

        def sem(n):
            sems.append(nc.alloc_semaphore(f"{name}_{n}"))
            return sems[-1]

        yield ctx, sb, ps, sem
    nc.clear_and_free_semaphores(sems)
    nc.all_engine_barrier()


class Step:

    def __init__(self, sem, base=0):
        self.sem, self.base, self.k = sem, base, 0

    def inc(self, ins):
        self.k += 1
        ins.then_inc(self.sem, 1)
        return self.k


def split_weights(nc, sem, name, jobs):
    PIECE = 2048
    pieces = []
    for src, hi, lo in jobs:
        for c in range(0, src.shape[1], PIECE):
            e = min(c + PIECE, src.shape[1])
            pieces.append((src[:, c:e], hi[:, c:e], lo[:, c:e], e - c))
    with ExitStack() as inner:
        stage = inner.enter_context(nc.sbuf_tensor(f"{name}_stage", [P, 2, PIECE], F32))
        loaded = [sem(f"w_loaded{i}") for i in range(2)]
        hi_done, lo_done = sem("w_hi_done"), sem("w_lo_done")
        block = inner.enter_context(nc.Block())

        @block.sync
        def _(sp):
            for i, (src, _, _, w) in enumerate(pieces):
                if i >= 2:
                    sp.wait_ge(lo_done, i - 1)
                sp.dma_start(stage[:, i % 2, 0:w], src).then_inc(loaded[i % 2], 16)

        @block.scalar
        def _(act):
            for i, (_, hi, _, w) in enumerate(pieces):
                act.wait_ge(loaded[i % 2], 16 * (i // 2 + 1))
                act.activation(hi, stage[:, i % 2, 0:w], ACT.Copy).then_inc(hi_done, 1)

        @block.vector
        def _(dve):
            for i, (_, hi, lo, w) in enumerate(pieces):
                dve.wait_ge(loaded[i % 2], 16 * (i // 2 + 1))
                dve.wait_ge(hi_done, i + 1)
                dve.tensor_tensor(lo, stage[:, i % 2, 0:w], f32(hi), ALU.subtract).then_inc(lo_done, 1)


def rows(w, width):
    return [w[k * P:(k + 1) * P, 0:width] for k in range(w.shape[0] // P)]


def weight(nc, ctx, name, kt, width):
    hi = ctx.enter_context(nc.sbuf_tensor(f"{name}_hi", [P, kt, width], F32R))
    lo = ctx.enter_context(nc.sbuf_tensor(f"{name}_lo", [P, kt, width], F32R))
    return hi, lo


def weight_jobs(w, dram):
    return [(src, w[0][:, k, :], w[1][:, k, :]) for k, src in enumerate(rows(dram, dram.shape[1]))]


def project(nc, name, x, tokens, weights, outs, ln=None):
    RING = 4
    full, rest = divmod(tokens, NB)
    rest_pad = -(-rest // P) * P
    BLOCKS = full + (rest > 0)
    LOOPS = (full - 1) // 2

    def products(width):
        found = []
        for src, wname, kind, dst in outs:
            if kind == "heads":
                found += [(src, wname, kind, dst, t) for t in range(width // P)]
            else:
                found += [(src, wname, kind, dst, m) for m in range(weights[wname].shape[1] // P)]
        return found

    STORE = 16 * (P // outs[0][3].shape[3] if outs[0][2] == "items" else 1)
    R = len(products(NB))
    uses = [len(range(s, R, RING)) for s in range(RING)]

    if ln is None:
        XL, NDVE, XH, NACT = 1, 1, 1, 1
        XT_READ = XL
    else:
        XL, XC, SQL, RSTD, XN, Z, ZL = 1, 2, 3, 4, 5, 5 + KT, 6 + KT
        XH, SQ, SQH, STD, ZH = 1, 2, 3, 4, 5
        NDVE, NACT = ZL, ZH
        XT_READ = XC

    with phase(nc, name) as (ctx, sb, ps, sem):
        W = {n: weight(nc, ctx, f"{name}_{n}", KT, w.shape[1]) for n, w in weights.items()}
        split_weights(nc, sem, name, [j for n, w in weights.items() for j in weight_jobs(W[n], w)])

        xt = [sb(f"xt{i}", [P, KT, NB], F32) for i in range(2)]
        raw = [(sb(f"xh{i}", [P, KT, NB], F32R), sb(f"xl{i}", [P, KT, NB], F32R)) for i in range(2)]
        if ln is not None:
            xc, sq = sb("xc", [P, KT, NB], F32), sb("sq", [P, KT, NB], F32)
            sqh, sql = sb("sqh", [P, KT, NB], F32R), sb("sql", [P, KT, NB], F32R)
            normed = [(sb(f"zh{i}", [P, KT, NB], F32R), sb(f"zl{i}", [P, KT, NB], F32R)) for i in range(2)]
            std, rstd = sb("std", [P, NB], F32), sb("rstd", [P, NB], F32)
            gb = sb("gb", [P, 2, KT], F32)
            eps = sb("eps", [P, 1], F32)
            inv_d, inv_dr = sb("inv_d", [P, P], F32), sb("inv_dr", [P, P], F32R)
            mean, var = ps("mean", [P, NB]), ps("var", [P, NB])
        out = [sb(f"out{i}", [P, 1024], F32R) for i in range(RING)]
        prod = [ps(f"prod{i}", [P, NB]) for i in range(RING)]

        x_loaded = [sem(f"x_loaded{i}") for i in range(2)]
        const_loaded, consts_done = sem("const_loaded"), sem("consts_done")
        dve_steps, act_steps, stats_done = sem("dve_steps"), sem("act_steps"), sem("stats_done")
        prod_done = [sem(f"prod_done{i}") for i in range(RING)]
        hi_done = [sem(f"hi_done{i}") for i in range(RING)]
        lo_done = [sem(f"lo_done{i}") for i in range(RING)]
        stored = [sem(f"stored{i}") for i in range(RING)]

        def width(n):
            return (rest, rest_pad) if isinstance(n, int) and n == full else (NB, NB)

        def blocks(eng):
            with eng.Fori(0, LOOPS) as i:
                yield i * 2, 0, i, True, True
                yield i * 2 + 1, 1, i, True, True
            for n in range(2 * LOOPS, BLOCKS):
                yield n, n % 2, n // 2, n + 1 < BLOCKS, n + 2 < BLOCKS

        def slot(n, i):
            return i % RING, n * uses[i % RING] + i // RING

        def halves(s, kind, dst, wp):
            if kind != "heads":
                return out[s][:, 0:wp], out[s][:, NB:NB + wp], prod[s][:, 0:wp]
            H, hd = dst.shape[0], dst.shape[3] // 2
            o = out[s][:, 0:H * 2 * hd].rearrange("p (h d) -> p h d", h=H)
            return o[:, :, 0:hd], o[:, :, hd:2 * hd], prod[s][:, 0:H * hd].rearrange("p (h d) -> p h d", h=H)

        def interleave(n, j, more, stages, do_product):
            todo = list(stages) if more else []
            made = products(width(n)[1])
            for i, p in enumerate(made):
                while todo and todo[0][0] * len(made) <= i:
                    todo.pop(0)[1](n + 1, 1 - j)
                do_product(n, j, i, *p)
            for _, f in todo:
                f(n + 1, 1 - j)

        block = ctx.enter_context(nc.Block())

        @block.sync
        def _(sp):
            if ln is not None:
                sp.dma_start(gb[:, 0, :], ln[0][:, :]).then_inc(const_loaded, 16)
                sp.dma_start(gb[:, 1, :], ln[1][:, :]).then_inc(const_loaded, 16)

            def load(n, j):
                w = width(n)[0]
                sp.dma_start(xt[j][:, :, 0:w],
                             x.rearrange("(k p) t -> p k t", p=P)[:, :, bass.ds(n * NB, w)]).then_inc(x_loaded[j], 16)

            def store(n, j, i, src, wn, kind, dst, m):
                s, before = slot(n, i)
                wp = width(n)[1]
                sp.wait_ge(lo_done[s], before + 1)
                if kind == "rows":
                    pairs = [(dst[:, m * P:(m + 1) * P, bass.ds(n * NB, wp)].rearrange("s p c -> p s c"), slice(0, P))]
                elif kind == "items":
                    hd = dst.shape[3]
                    pairs = [(dst[m * P // hd + g, bass.ds(n, 1)].rearrange("o s r c -> r (o s) c"),
                              slice(g * hd, (g + 1) * hd)) for g in range(P // hd)]
                else:
                    H, hd2 = dst.shape[0], dst.shape[3]
                    to = dst[:, :, bass.ds(n * (NB // P) + m, 1), :].rearrange("h p t d -> p h (t d)")
                    sp.dma_start(to, f32(out[s][:, 0:H * hd2]).rearrange("p (h d) -> p h d", h=H)).then_inc(stored[s], 16)
                    return
                of = f32(out[s][:, 0:2 * NB]).rearrange("p (s c) -> p s c", s=2)
                for to, at in pairs:
                    sp.dma_start(to, of[at, :, 0:wp]).then_inc(stored[s], 16)

            load(0, 0)
            load(1, 1)
            for n, j, _, more, two in blocks(sp):
                if two:
                    sp.wait_ge(dve_steps, n * NDVE + XT_READ)
                    load(n + 2, j)
                for i, p in enumerate(products(width(n)[1])):
                    store(n, j, i, *p)
            tail = len(products(rest_pad)) if rest else 0
            for s in range(RING):
                count = full * uses[s] + len(range(s, tail, RING))
                if count:
                    sp.wait_ge(stored[s], STORE * count)

        @block.scalar
        def _(act):
            def split(n, j):
                w = width(n)[0]
                act.wait_ge(x_loaded[j], (n + 2 - j) * 8)
                if not isinstance(n, int) or n > 1:
                    act.wait_ge(prod_done[(R - 1) % RING], (n - 1) * uses[(R - 1) % RING])
                act.activation(raw[j][0][:, :, 0:w], xt[j][:, :, 0:w], ACT.Copy).then_inc(act_steps, 1)

            def squares(n, j):
                w = width(n)[0]
                act.wait_ge(dve_steps, n * NDVE + XC)
                act.activation(sq[:, :, 0:w], xc[:, :, 0:w], ACT.Square).then_inc(act_steps, 1)
                act.wait_ge(act_steps, n * NACT + SQ)
                act.activation(sqh[:, :, 0:w], sq[:, :, 0:w], ACT.Copy).then_inc(act_steps, 1)

            def deviation(n, j):
                w = width(n)[0]
                act.wait_ge(stats_done, n * 2 + 2)
                act.activation(std[:, 0:w], var[:, 0:w], ACT.Sqrt, bias=eps[:, 0:1]).then_inc(act_steps, 1)

            def split_normed(n, j):
                w = width(n)[0]
                act.wait_ge(dve_steps, n * NDVE + Z)
                act.activation(normed[j][0][:, :, 0:w], xc[:, :, 0:w], ACT.Copy).then_inc(act_steps, 1)

            def evacuate(n, j, i, src, wn, kind, dst, m):
                s, before = slot(n, i)
                hi, _, y = halves(s, kind, dst, width(n)[1])
                act.wait_ge(prod_done[s], before + 1)
                act.wait_ge(stored[s], before * STORE)
                act.activation(hi, y, ACT.Copy).then_inc(hi_done[s], 1)

            stages = [(0, split)]
            if ln is not None:
                act.wait_ge(consts_done, 3)
                stages += [(0.25, squares), (0.55, deviation), (0.8, split_normed)]
            for _, f in stages:
                f(0, 0)
            for n, j, _, more, _ in blocks(act):
                interleave(n, j, more, stages, evacuate)

        @block.vector
        def _(dve):
            def step(n, k, ins, wait=True):
                ins.then_inc(dve_steps, 1)
                if wait:
                    dve.wait_ge(dve_steps, n * NDVE + k)

            def split(n, j):
                w, wp = width(n)
                if wp > w:
                    dve.wait_ge(prod_done[(R - 1) % RING], (n - 1) * uses[(R - 1) % RING])
                    for t in raw[j] + (normed[j] if ln is not None else ()):
                        dve.memset(f32(t[:, :, w:wp]), 0.0)
                dve.wait_ge(act_steps, n * NACT + XH)
                step(n, XL, dve.tensor_tensor(raw[j][1][:, :, 0:w], xt[j][:, :, 0:w], f32(raw[j][0][:, :, 0:w]),
                                              ALU.subtract), False)

            def centre(n, j):
                w = width(n)[0]
                dve.wait_ge(stats_done, n * 2 + 1)
                step(n, XC, dve.tensor_tensor(xc[:, :, 0:w], xt[j][:, :, 0:w],
                                              mean[:, 0:w].unsqueeze(1).to_broadcast([P, KT, w]), ALU.subtract), False)

            def split_squares(n, j):
                w = width(n)[0]
                dve.wait_ge(act_steps, n * NACT + SQH)
                step(n, SQL, dve.tensor_tensor(sql[:, :, 0:w], sq[:, :, 0:w], f32(sqh[:, :, 0:w]), ALU.subtract), False)

            def norm(n, j):
                w = width(n)[0]
                dve.wait_ge(act_steps, n * NACT + STD)
                step(n, RSTD, dve.reciprocal(rstd[:, 0:w], std[:, 0:w]))
                step(n, XN, dve.tensor_tensor(sq[:, :, 0:w], xc[:, :, 0:w],
                                              rstd[:, 0:w].unsqueeze(1).to_broadcast([P, KT, w]), ALU.mult))
                for k in range(KT):
                    step(n, XN + k + 1, dve.tensor_scalar(xc[:, k, 0:w], sq[:, k, 0:w], gb[:, 0, k:k + 1],
                                                          gb[:, 1, k:k + 1], ALU.mult, ALU.add), False)

            def split_normed(n, j):
                w = width(n)[0]
                dve.wait_ge(act_steps, n * NACT + ZH)
                step(n, ZL, dve.tensor_tensor(normed[j][1][:, :, 0:w], xc[:, :, 0:w], f32(normed[j][0][:, :, 0:w]),
                                              ALU.subtract), False)

            def evacuate(n, j, i, src, wn, kind, dst, m):
                s, before = slot(n, i)
                hi, lo, y = halves(s, kind, dst, width(n)[1])
                dve.wait_ge(hi_done[s], before + 1)
                dve.tensor_tensor(lo, y, f32(hi), ALU.subtract).then_inc(lo_done[s], 1)

            stages = [(0, split)]
            if ln is not None:
                dve.memset(eps[:], LN_EPS).then_inc(consts_done, 1)
                dve.memset(inv_d[:], 1.0 / D).then_inc(consts_done, 1)
                dve.wait_ge(consts_done, 2)
                dve.tensor_copy(inv_dr[:], inv_d[:]).then_inc(consts_done, 1)
                dve.wait_ge(const_loaded, 32)
                stages += [(0.25, centre), (0.4, split_squares), (0.6, norm), (0.85, split_normed)]
            for _, f in stages:
                f(0, 0)
            for n, j, _, more, _ in blocks(dve):
                interleave(n, j, more, stages, evacuate)

        @block.tensor
        def _(pe):
            def statistic(stat, parts, n, w):
                for i in range(2 * KT):
                    mm = pe.matmul(stat[:, 0:w], inv_dr[:], parts[i // KT][:, i % KT, 0:w],
                                   start=(i == 0), stop=(i == 2 * KT - 1))
                mm.then_inc(stats_done, 1)

            def find_mean(n, j):
                pe.wait_ge(dve_steps, n * NDVE + XL)
                statistic(mean, raw[j], n, width(n)[0])

            def find_variance(n, j):
                pe.wait_ge(dve_steps, n * NDVE + SQL)
                statistic(var, (sqh, sql), n, width(n)[0])

            def product(n, j, i, src, wn, kind, dst, m):
                s, before = slot(n, i)
                wp = width(n)[1]
                if i == 0:
                    pe.wait_ge(dve_steps, n * NDVE + NDVE)
                pe.wait_ge(lo_done[s], before)
                xs, ws = (raw if src == "raw" else normed)[j], W[wn]
                terms = [(k, a, b) for k in range(KT) for a, b in ((0, 0), (0, 1), (1, 0))]
                for t, (k, a, b) in enumerate(terms):
                    if kind == "heads":
                        c = ws[a].shape[2]
                        o, l, r = prod[s][:, 0:c], xs[b][:, k, m * P:(m + 1) * P], ws[a][:, k, :]
                    else:
                        o, l, r = prod[s][:, 0:wp], ws[a][:, k, m * P:(m + 1) * P], xs[b][:, k, 0:wp]
                    mm = pe.matmul(o, l, r, start=(t == 0), stop=(t == len(terms) - 1))
                mm.then_inc(prod_done[s], 1)

            stages = []
            if ln is not None:
                pe.wait_ge(consts_done, 3)
                stages = [(0.2, find_mean), (0.5, find_variance)]
            for _, f in stages:
                f(0, 0)
            for n, j, _, more, _ in blocks(pe):
                interleave(n, j, more, stages, product)



GROUPS = ST // 2
RINGS = [0, 1, 2, 3, 4, 5] * (GROUPS // 6) + [6]
LAST_RING = RINGS[-1]
NRING = LAST_RING + 1
LAG = 4
SCORES = [([0, 1, 2] * ST)[:ST], ([0, 2, 1] * ST)[:ST]]
CHUNKS = 4
CHUNK = -(-S // (2 * CHUNKS)) * 2
UNITS = (NB // P) * CHUNKS
UNITS_AT = {0: [0, 1], 1: [2], 2: [3], 3: [4, 5], 4: [6], 5: [7], 6: [8, 9], 7: [10], 8: [11], 9: [12, 13],
            10: [14], 11: [15]}
ROW_AT = 12
POOL_LO = (1, 3, 5, 7, 9, 11)
DVE_HI = (4, 10)
QB = T // NB


class Item:

    def __init__(self, pair, k, qb, j, half, prev_k=None, next_k=None, first=False, last=False, final_head=False,
                 last_two=False):
        self.final_head, self.last_two = final_head, last_two
        self.pair, self.k, self.qb, self.j = pair, k, qb, j
        self.h = pair * 2 + k
        self.n = self.h * QB + qb
        self.use = self.h * (QB // 2) + half
        self.prev_use = self.use if j == 1 else self.use - 1
        self.next_use = self.use if j == 0 else self.use + 1
        self.prev_k = k if prev_k is None else prev_k
        self.next_k = k if next_k is None else next_k
        self.starts_head, self.ends_head = prev_k is not None, next_k is not None
        self.first, self.last = first, last


def attention(nc, name, H, hd, q, k, v, acc_out):
    SCALE = float(hd) ** -0.5
    ROW = 96
    C = ROW + 1
    M = 96
    PAIRS = H // 2
    LAST_KEYS = S - (ST - 1) * P

    with phase(nc, name) as (ctx, sb, ps, sem):

        kt = [sb(f"k{i}", [C, SPAD], F32R) for i in range(2)]
        vt = [sb(f"v{i}", [P, ST, M], F32R) for i in range(2)]
        qt = [sb(f"q{i}", [C, NB], F32R) for i in range(2)]
        qm = [sb(f"qm{i}", [ROW, NB], F32R) for i in range(2)]
        prob = [sb(f"prob{i}", [P, 2 * NB], F32) for i in range(NRING)]
        phi = [sb(f"phi{i}", [P, 2 * NB], F32R) for i in range(NRING)]
        plo = [sb(f"plo{i}", [P, 2 * NB], F32R) for i in range(NRING)]
        acc_sb = [sb(f"acc_sb{i}", [M, NB], F32) for i in range(2)]
        maxes = sb("maxes", [P, NB // P, CHUNKS], F32)
        negmax = sb("negmax", [P, NB // P], F32)
        ident = sb("ident", [P, P], F32)

        score = [ps(f"score{i}", [P, NB]) for i in range(3)]
        mscore = [ps(f"mscore{i}", [P, 2 * NB]) for i in range(2)]
        acc = ps("acc", [M, NB])

        k_loaded = [sem(f"k_loaded{i}") for i in range(2)]
        v_loaded = [sem(f"v_loaded{i}") for i in range(2)]
        q_loaded = [sem(f"q_loaded{i}") for i in range(2)]
        qm_loaded = [sem(f"qm_loaded{i}") for i in range(2)]
        filled, ident_done = sem("filled"), sem("ident_done")
        score_done = [sem(f"score_done{i}") for i in range(3)]
        exp_done = [sem(f"exp_done{i}") for i in range(NRING)]
        hi_done = [sem(f"hi_done{i}") for i in range(NRING)]
        lo_done = [sem(f"lo_done{i}") for i in range(NRING)]
        pv_done = [sem(f"pv_done{i}") for i in range(NRING)]
        unit_done, unit_read = sem("unit_done"), sem("unit_read")
        neg_done, row_done, row_copied = sem("neg_done"), sem("row_done"), sem("row_copied")
        acc_copied = sem("acc_copied")
        acc_stored = [sem(f"acc_stored{i}") for i in range(2)]

        def items(eng):
            def pair(p, first, last):
                for kk in range(2):
                    final = last and kk == 1
                    yield Item(p, kk, 0, 0, 0, prev_k=1 - kk, first=first and kk == 0, final_head=final)
                    with eng.Fori(0, QB // 2 - 1 - final) as i:
                        yield Item(p, kk, i * 2 + 1, 1, i)
                        yield Item(p, kk, i * 2 + 2, 0, i + 1)
                    if final:
                        yield Item(p, kk, QB - 3, 1, QB // 2 - 2)
                        yield Item(p, kk, QB - 2, 0, QB // 2 - 1, last_two=True)
                    yield Item(p, kk, QB - 1, 1, QB // 2 - 1, next_k=1 - kk, last=final, last_two=final)

            yield from pair(0, True, False)
            with eng.Fori(1, PAIRS - 1) as p:
                yield from pair(p, False, False)
            yield from pair(PAIRS - 1, False, True)

        def steps(it):
            return range(GROUPS + LAG) if it.last else range(GROUPS)

        def ring_uses(it, g):
            return it.n * RINGS.count(RINGS[g]) + RINGS[:g].count(RINGS[g])

        def score_buffer(j, use, t):
            b = SCORES[j][t]
            both = SCORES[0].count(b) + SCORES[1].count(b)
            return b, use * both + j * SCORES[0].count(b) + SCORES[j][:t].count(b)

        def score_read(it, t):
            b = SCORES[it.j][t]
            same = [u for u in range(t) if SCORES[it.j][u] == b]
            if same:
                g, odd = divmod(same[-1], 2)
                return RINGS[g], ring_uses(it, g) * 2 + odd + 1
            if it.first:
                return None
            g, odd = divmod(max(u for u in range(ST) if SCORES[1 - it.j][u] == b), 2)
            r = RINGS[g]
            return r, (it.n * RINGS.count(r) - RINGS[g:].count(r)) * 2 + odd + 1

        def lagged(it, s, lag):
            g = s - lag
            if g >= GROUPS or (g < 0 and it.first):
                return None
            if g >= 0:
                return g, RINGS[g], ring_uses(it, g), it.k
            g += GROUPS
            r = RINGS[g]
            return g, r, it.n * RINGS.count(r) - RINGS[g:].count(r), it.prev_k

        FILLS, REFILLS = [], []
        for i in range(2):
            FILLS.append((f32(vt[i][:]), 1.0))
            REFILLS.append((f32(vt[i][:, ST - 1, 2 * hd:M]), 0.0))
            FILLS += [(f32(kt[i][ROW:C, 0:S]), 1.0), (f32(kt[i][ROW:C, S:SPAD]), 0.0)]
            for at in range(3 * hd // 32 * 32, ROW, 32):
                FILLS += [(f32(x[i][at:at + 32, :]), 0.0) for x in (kt, qt, qm)]
        TOP = [(f32(vt[i][0:LAST_KEYS, ST - 1, 2 * hd:M]), 1.0) for i in range(2)]
        NFILL = len(FILLS) + len(REFILLS) + len(TOP)

        q_items = q.rearrange("h b s r c -> (h b) s r c")
        block = ctx.enter_context(nc.Block())

        @block.sync
        def _(sp):
            def load_kv(h, kk):
                rows = bass.ds(h * hd, hd)
                for at, half in ((0, 0), (hd, 1), (2 * hd, 0)):
                    sp.dma_start(f32(kt[kk][at:at + hd, :]), k[half, rows, :]).then_inc(k_loaded[kk], 16)
                sp.dma_start(f32(vt[kk][:, :, 0:2 * hd]),
                             v[bass.ds(h, 1)].rearrange("o p t d -> p (o t) d")).then_inc(v_loaded[kk], 16)

            def load_q(tile, n, loaded):
                for at, half in ((0, 0), (hd, 0), (2 * hd, 1)):
                    sp.dma_start(f32(tile[at:at + hd, :]),
                                 q_items[bass.ds(n, 1), half].rearrange("o r c -> (o r) c")).then_inc(loaded, 16)

            def store(h, qb, j, n):
                sp.wait_ge(acc_copied, n + 1)
                sp.dma_start(acc_out[bass.ds(h, 1), :, bass.ds(qb * NB, NB)].rearrange("o r c -> (o r) c"),
                             acc_sb[j][0:3 * hd, :]).then_inc(acc_stored[j], 16)

            sp.wait_ge(filled, NFILL)
            load_kv(0, 0)
            load_q(qm[0], 0, qm_loaded[0])
            load_q(qm[1], 1, qm_loaded[1])
            load_q(qt[0], 0, q_loaded[0])
            load_kv(1, 1)
            for it in items(sp):
                if not it.last:
                    if not it.first:
                        b, before = score_buffer(1 - it.j, it.prev_use, ST - 1)
                        sp.wait_ge(score_done[b], before + 1)
                    load_q(qt[1 - it.j], it.n + 1, q_loaded[1 - it.j])
                if not it.last_two:
                    sp.wait_ge(neg_done, it.n + 1)
                    load_q(qm[it.j], it.n + 2, qm_loaded[it.j])
                if not it.first:
                    if it.starts_head:
                        store(it.h - 1, QB - 1, 1 - it.j, it.n - 1)
                    else:
                        store(it.h, it.qb - 1, 1 - it.j, it.n - 1)
                if it.starts_head and not it.first and not it.final_head:
                    sp.wait_ge(pv_done[LAST_RING], it.h * QB)
                    load_kv(it.h + 1, 1 - it.k)
                if it.last:
                    store(it.h, it.qb, it.j, it.n)
            for j in range(2):
                sp.wait_ge(acc_stored[j], H * (QB // 2) * 16)

        @block.gpsimd
        def _(pool):
            pool.memset(ident[:], 0.0).then_inc(ident_done, 1)
            pool.wait_ge(ident_done, 1)
            pool.affine_select(out=ident[:], in_=ident[:], compare_op=ALU.not_equal, fill=1.0, base=0,
                               pattern=[[-1, P]], channel_multiplier=1).then_inc(ident_done, 1)
            for it in items(pool):
                for s in steps(it):
                    if (x := lagged(it, s, 2)) and x[0] in POOL_LO:
                        _, r, uses, _ = x
                        pool.wait_ge(hi_done[r], uses + 1)
                        pool.tensor_tensor(plo[r][:], prob[r][:], f32(phi[r][:]), ALU.subtract).then_inc(lo_done[r], 1)

        @block.scalar
        def _(act):
            def copy_row(j, n):
                act.wait_ge(row_done, n + 1)
                act.activation(qt[j][ROW:C, :], mscore[0][0:1, 0:NB], ACT.Copy).then_inc(row_copied, 1)

            def copy_acc(n, j, use):
                act.wait_ge(pv_done[LAST_RING], n + 1)
                act.wait_ge(acc_stored[j], use * 16)
                act.activation(acc_sb[j][0:3 * hd, :], acc[0:3 * hd, :], ACT.Copy).then_inc(acc_copied, 1)

            copy_row(0, 0)
            for it in items(act):
                for s in steps(it):
                    if s < GROUPS:
                        r = RINGS[s]
                        act.wait_ge(pv_done[r], ring_uses(it, s))
                        for i in range(2):
                            b, before = score_buffer(it.j, it.use, 2 * s + i)
                            act.wait_ge(score_done[b], before + 1)
                            act.activation(prob[r][:, i * NB:(i + 1) * NB], score[b][:], ACT.Exp,
                                           scale=SCALE).then_inc(exp_done[r], 1)
                    if s == ROW_AT and not it.last:
                        copy_row(1 - it.j, it.n + 1)
                    if (x := lagged(it, s, 1)) and x[0] not in DVE_HI:
                        _, r, uses, _ = x
                        act.wait_ge(exp_done[r], uses * 2 + 2)
                        act.activation(phi[r][:], prob[r][:], ACT.Copy).then_inc(hi_done[r], 1)
                    if s == LAG - 1 and not it.first:
                        copy_acc(it.n - 1, 1 - it.j, it.prev_use)
                    if s == GROUPS + LAG - 1:
                        copy_acc(it.n, it.j, it.use)

        @block.vector
        def _(dve):
            def maximum(n, u):
                t, c = divmod(u, CHUNKS)
                w = min(CHUNK, S - c * CHUNK)
                dve.wait_ge(unit_done, n * UNITS + u + 1)
                dve.tensor_reduce(maxes[:, t, c:c + 1], mscore[u % 2][:, 0:w], AX.X, ALU.max).then_inc(unit_read, 1)
                if u == UNITS - 1:
                    dve.wait_ge(unit_read, n * UNITS + UNITS)
                    dve.tensor_reduce(negmax[:], maxes[:], AX.X, ALU.max, negate=True).then_inc(neg_done, 1)

            for ap, value in FILLS:
                dve.memset(ap, value).then_inc(filled, 1)
            dve.wait_ge(filled, len(FILLS))
            for ap, value in REFILLS:
                dve.memset(ap, value).then_inc(filled, 1)
            dve.wait_ge(filled, len(FILLS) + len(REFILLS))
            for ap, value in TOP:
                dve.memset(ap, value).then_inc(filled, 1)
            for u in range(UNITS):
                maximum(0, u)
            for it in items(dve):
                for s in steps(it):
                    if not it.last:
                        for u in UNITS_AT.get(s, ()):
                            maximum(it.n + 1, u)
                    if (x := lagged(it, s, 1)) and x[0] in DVE_HI:
                        _, r, uses, _ = x
                        dve.wait_ge(exp_done[r], uses * 2 + 2)
                        dve.tensor_copy(phi[r][:], prob[r][:]).then_inc(hi_done[r], 1)
                    if (x := lagged(it, s, 2)) and x[0] not in POOL_LO:
                        _, r, uses, _ = x
                        dve.wait_ge(hi_done[r], uses + 1)
                        dve.tensor_tensor(plo[r][:], prob[r][:], f32(phi[r][:]), ALU.subtract).then_inc(lo_done[r], 1)

        @block.tensor
        def _(pe):
            def unit(n, j, kk, u):
                t, c = divmod(u, CHUNKS)
                lo, hi = c * CHUNK, min((c + 1) * CHUNK, S)
                if not (isinstance(n, int) and n == 0 and u < 2):
                    pe.wait_ge(unit_read, n * UNITS + u - 1)
                for at in range(lo, hi, NB):
                    e = min(at + NB, hi)
                    mm = pe.matmul(mscore[u % 2][:, at - lo:e - lo], qm[j][:, t * P:(t + 1) * P],
                                   kt[kk][0:ROW, at:e], start=True, stop=True)
                mm.then_inc(unit_done, 1)

            def make_row(n):
                pe.wait_ge(neg_done, n + 1)
                for t in range(NB // P):
                    mm = pe.matmul(mscore[0][0:1, t * P:(t + 1) * P], negmax[:, t:t + 1], ident[:], start=True, stop=True)
                mm.then_inc(row_done, 1)

            pe.wait_ge(ident_done, 2)
            pe.wait_ge(k_loaded[0], 48)
            pe.wait_ge(qm_loaded[0], 48)
            for u in range(UNITS):
                unit(0, 0, 0, u)
            make_row(0)
            def scores(it, t):
                if x := score_read(it, t):
                    pe.wait_ge(exp_done[x[0]], x[1])
                b, _ = score_buffer(it.j, it.use, t)
                pe.matmul(score[b][:], kt[it.k][:, t * P:(t + 1) * P], qt[it.j][:],
                          start=True, stop=True).then_inc(score_done[b], 1)

            for it in items(pe):
                for s in steps(it):
                    if s == 0:
                        pe.wait_ge(q_loaded[it.j], (it.use + 1) * 48)
                        pe.wait_ge(row_copied, it.n + 1)
                    if s < GROUPS:
                        scores(it, 2 * s)
                    if not it.last:
                        if s == 0:
                            pe.wait_ge(qm_loaded[1 - it.j], (it.next_use + 1) * 48)
                            if it.ends_head:
                                pe.wait_ge(k_loaded[it.next_k], (it.pair + it.k + 1) * 48)
                        for u in UNITS_AT.get(s, ()):
                            unit(it.n + 1, 1 - it.j, it.next_k, u)
                        if s == ROW_AT:
                            make_row(it.n + 1)
                    if s < GROUPS:
                        scores(it, 2 * s + 1)
                    if x := lagged(it, s, LAG):
                        g, r, uses, kk = x
                        if g == 0:
                            if it.starts_head:
                                pe.wait_ge(v_loaded[it.k], (it.pair + 1) * 16)
                            pe.wait_ge(acc_copied, it.n)
                        pe.wait_ge(hi_done[r], uses + 1)
                        pe.wait_ge(lo_done[r], uses + 1)
                        for i in range(2):
                            for part in (phi, plo):
                                t = 2 * g + i
                                mm = pe.matmul(acc[:], vt[kk][:, t, :], part[r][:, i * NB:(i + 1) * NB],
                                               start=(t == 0 and part is phi), stop=(t == ST - 1 and part is plo))
                        mm.then_inc(pv_done[r], 1)



def tail(nc, name, H, hd, acc, x, wo, bo, w1, b1, func, w2, b2, out):
    KO = H * hd // P
    HT = P // hd
    F = w1.shape[1]
    FT = F // P

    with phase(nc, name) as (ctx, sb, ps, sem):

        WO, W1, W2 = weight(nc, ctx, f"{name}_wo", KO, D), weight(nc, ctx, f"{name}_w1", KT, F), weight(nc, ctx, f"{name}_w2", FT, D)
        split_weights(nc, sem, name, weight_jobs(WO, wo) + weight_jobs(W1, w1) + weight_jobs(W2, w2))

        bias1 = sb("bias1", [P, FT], F32)
        bias2 = sb("bias2", [P, KT], F32)
        biaso = sb("biaso", [P, KT], F32)
        part = sb("part", [P, 3, KO, NB], F32)
        X = sb("X", [P, KT, NB], F32)
        y = sb("y", [P, KT, NB], F32) if KO < KT else part[:, 1]
        xh, xl = sb("xh", [P, KT, NB], F32R), sb("xl", [P, KT, NB], F32R)
        h = [sb(f"h{i}", [P, NB], F32) for i in range(2)]
        hh = [sb(f"hh{i}", [P, NB], F32R) for i in range(2)]
        hl = [sb(f"hl{i}", [P, NB], F32R) for i in range(2)]
        hp = [ps(f"hp{i}", [P, NB]) for i in range(2)]
        yp = [ps(f"yp{m}", [P, NB]) for m in range(KT)]

        const_loaded, loaded, stored = sem("const_loaded"), sem("acts_loaded"), sem("stored")
        dve_steps = sem("dve_steps")
        wo_done = sem("wo_done")
        hp_done = [sem(f"hp_done{i}") for i in range(2)]
        act_done = [sem(f"act_done{i}") for i in range(2)]
        hh_done = [sem(f"hh_done{i}") for i in range(2)]
        hl_done = [sem(f"hl_done{i}") for i in range(2)]
        used = [sem(f"used{i}") for i in range(2)]
        NCONST = 48 if bo is not None else 32
        NLOAD = 3 * H + 1
        O_LO, X_DONE, X_LO, NDVE = 5, 5 + KT, 7 + KT, 7 + 2 * KT
        HALF = FT // 2
        block = ctx.enter_context(nc.Block())

        @block.sync
        def _(sp):
            sp.dma_start(bias1[:], b1[:, :]).then_inc(const_loaded, 16)
            sp.dma_start(bias2[:], b2[:, :]).then_inc(const_loaded, 16)
            if bo is not None:
                sp.dma_start(biaso[:], bo[:, :]).then_inc(const_loaded, 16)
            with sp.Fori(0, T // NB) as n:
                cols = bass.ds(n * NB, NB)
                sp.wait_ge(stored, n * 16)
                for i in range(3):
                    for hx in range(H):
                        at = hx % HT * hd
                        sp.dma_start(part[at:at + hd, i, hx // HT, :], acc[hx, i * hd:(i + 1) * hd, cols]).then_inc(loaded, 16)
                sp.dma_start(X[:], x.rearrange("(k p) t -> p k t", p=P)[:, :, cols]).then_inc(loaded, 16)
                sp.wait_ge(dve_steps, n * NDVE + NDVE)
                sp.dma_start(out.rearrange("(k p) t -> p k t", p=P)[:, :, cols], y[:]).then_inc(stored, 16)
            sp.wait_ge(stored, T // NB * 16)

        @block.vector
        def _(dve):
            dve.wait_ge(const_loaded, NCONST)
            with dve.Fori(0, T // NB) as n:
                base = n * NDVE
                step = Step(dve_steps)

                def chain(ins):
                    step.inc(ins)
                    dve.wait_ge(dve_steps, base + step.k)

                dve.wait_ge(loaded, n * (NLOAD * 16) + NLOAD * 16)
                chain(dve.tensor_tensor(part[:, 0], part[:, 0], part[:, 1], ALU.add))
                chain(dve.reciprocal(part[:, 2], part[:, 2]))
                chain(dve.tensor_tensor(part[:, 0], part[:, 0], part[:, 2], ALU.mult))
                dve.wait_ge(hp_done[1], n * HALF)
                chain(dve.tensor_copy(xh[:, 0:KO], part[:, 0]))
                chain(dve.tensor_tensor(xl[:, 0:KO], part[:, 0], f32(xh[:, 0:KO]), ALU.subtract))
                dve.wait_ge(wo_done, n + 1)
                for m in range(KT):
                    if bo is not None:
                        step.inc(dve.scalar_tensor_tensor(X[:, m], yp[m][:], biaso[:, m:m + 1], X[:, m], ALU.add, ALU.add))
                    else:
                        step.inc(dve.tensor_tensor(X[:, m], yp[m][:], X[:, m], ALU.add))
                dve.wait_ge(dve_steps, base + step.k)
                chain(dve.tensor_copy(xh[:], X[:]))
                chain(dve.tensor_tensor(xl[:], X[:], f32(xh[:]), ALU.subtract))
                for m in range(FT):
                    b, before = m % 2, n * HALF + m // 2
                    dve.wait_ge(hh_done[b], before + 1)
                    dve.wait_ge(used[b], before)
                    dve.tensor_tensor(hl[b][:], h[b][:], f32(hh[b][:]), ALU.subtract).then_inc(hl_done[b], 1)
                dve.wait_ge(used[1], n * HALF + HALF)
                for m in range(KT):
                    step.inc(dve.scalar_tensor_tensor(y[:, m], yp[m][:], bias2[:, m:m + 1], X[:, m], ALU.add, ALU.add))
                assert step.k == NDVE

        @block.scalar
        def _(act):
            act.wait_ge(const_loaded, NCONST)
            with act.Fori(0, T // NB) as n:
                for m in range(FT):
                    b, before = m % 2, n * HALF + m // 2
                    act.wait_ge(hp_done[b], before + 1)
                    act.wait_ge(hl_done[b], before)
                    act.activation(h[b][:], hp[b][:], func, bias=bias1[:, m:m + 1]).then_inc(act_done[b], 1)
                    act.wait_ge(act_done[b], before + 1)
                    act.wait_ge(used[b], before)
                    act.activation(hh[b][:], h[b][:], ACT.Copy).then_inc(hh_done[b], 1)

        @block.tensor
        def _(pe):
            TERMS = ((0, 0), (0, 1), (1, 0))

            def use_hidden(n, m):
                b, before = m % 2, n * HALF + m // 2
                pe.wait_ge(hl_done[b], before + 1)
                for a, c in TERMS:
                    for d in range(KT):
                        mm = pe.matmul(yp[d][:], W2[a][:, m, d * P:(d + 1) * P], (hh, hl)[c][b][:],
                                       start=(m == 0 and (a, c) == (0, 0)), stop=(m == FT - 1 and (a, c) == (1, 0)))
                mm.then_inc(used[b], 1)

            with pe.Fori(0, T // NB) as n:
                pe.wait_ge(dve_steps, n * NDVE + O_LO)
                for d in range(KT):
                    for i, (k, a, c) in enumerate([(k, a, c) for k in range(KO) for a, c in TERMS]):
                        mm = pe.matmul(yp[d][:], WO[a][:, k, d * P:(d + 1) * P], (xh, xl)[c][:, k],
                                       start=(i == 0), stop=(i == 3 * KO - 1))
                mm.then_inc(wo_done, 1)
                pe.wait_ge(dve_steps, n * NDVE + X_LO)
                for m in range(FT):
                    b, before = m % 2, n * HALF + m // 2
                    pe.wait_ge(act_done[b], before)
                    for i, (k, a, c) in enumerate([(k, a, c) for k in range(KT) for a, c in TERMS]):
                        mm = pe.matmul(hp[b][:], W1[a][:, k, m * P:(m + 1) * P], (xh, xl)[c][:, k],
                                       start=(i == 0), stop=(i == 3 * KT - 1))
                    mm.then_inc(hp_done[b], 1)
                    if m:
                        use_hidden(n, m - 1)
                use_hidden(n, FT - 1)


def build(nc, a, out):
    L0, L1 = (8, 16), (16, 32)

    def scratch(n, shape):
        return nc.dram_tensor(n, shape, F32).ap()

    q, k, v, acc = [], [], [], []
    for i, (H, hd) in enumerate((L0, L1)):
        q.append(scratch(f"q{i}", [H, QB, 2, hd, NB]))
        k.append(scratch(f"k{i}", [2, H * hd, SPAD]))
        v.append(scratch(f"v{i}", [H, P, ST, 2 * hd]))
        acc.append(scratch(f"acc{i}", [H, 3 * hd, T]))
    x1 = scratch("x1", [D, T])
    ctx_t, x = a["ctx_1024"], a["x"]

    project(nc, "kv", ctx_t, S,
            {"k0": a["L0_xattn_W_k"], "v0": a["L0_xattn_W_v"], "k1": a["L1_xattn_Wkv"][:, 0:D], "v1": a["L1_xattn_Wkv"][:, D:2 * D]},
            [("raw", "k0", "rows", k[0]), ("raw", "v0", "heads", v[0]),
             ("ln", "k1", "rows", k[1]), ("ln", "v1", "heads", v[1])],
            ln=(a["L1_xattn_ln_kv_g"], a["L1_xattn_ln_kv_b"]))
    project(nc, "pq0", x, T, {"q0": a["L0_xattn_W_q"]}, [("raw", "q0", "items", q[0])])
    attention(nc, "a0", *L0, q[0], k[0], v[0], acc[0])
    tail(nc, "t0", *L0, acc[0], x, a["L0_xattn_W_o"], None, a["L0_xattn_w1"], a["L0_xattn_b1"], ACT.Relu,
         a["L0_xattn_w2"], a["L0_xattn_b2"], x1)
    project(nc, "pq1", x1, T, {"q1": a["L1_xattn_Wq"]}, [("ln", "q1", "items", q[1])],
            ln=(a["L1_xattn_ln_q_g"], a["L1_xattn_ln_q_b"]))
    attention(nc, "a1", *L1, q[1], k[1], v[1], acc[1])
    tail(nc, "t1", *L1, acc[1], x1, a["L1_xattn_Wo"], a["L1_xattn_bo"], a["L1_xattn_W1"], a["L1_xattn_b1"], ACT.Silu,
         a["L1_xattn_W2"], a["L1_xattn_b2"], out)


TRANSPOSED = {"x", "ctx_1024", "L0_xattn_w1", "L0_xattn_w2", "L1_xattn_Wq", "L1_xattn_Wkv", "L1_xattn_Wo",
              "L1_xattn_W1", "L1_xattn_W2"}


def kernel(**inputs):
    import numpy as np
    import concourse.bacc as bacc
    from concourse.bass_utils import run_bass_kernel_spmd

    nc = bacc.Bacc("TRN2", target_bir_lowering=False, num_devices=1)
    arrays, aps = {}, {}
    for name, value in inputs.items():
        a = np.asarray(value)
        if name in ("x", "ctx_1024"):
            a = a[0]
        if a.ndim == 1:
            a = a.reshape(-1, P)
        if name in TRANSPOSED or value.ndim == 1:
            a = a.T
        a = np.ascontiguousarray(a)
        arrays[f"in_{name}"] = a
        aps[name] = nc.dram_tensor(f"in_{name}", a.shape, mybir.dt.from_np(a.dtype), kind="ExternalInput").ap()
    out = nc.dram_tensor("out_t", (D, T), F32, kind="ExternalOutput").ap()
    build(nc, aps, out)
    r = run_bass_kernel_spmd(nc, [arrays], core_ids=[0])
    return np.ascontiguousarray(r.results[0]["out_t"].T)[None]
```

```python
from contextlib import ExitStack, contextmanager

import concourse.bass as bass
from concourse import mybir

F32 = mybir.dt.float32
F32R = mybir.dt.float32r
ALU = mybir.AluOpType
ACT = mybir.ActivationFunctionType
AX = mybir.AxisListType

P = 128
D = 512
KT = D // P
T = 4096
NB = 512
S = 3202
ST = -(-S // P)
SPAD = ST * P
LN_EPS = 1e-5


def f32(ap):
    return ap.bitcast(F32)


@contextmanager
def phase(nc, name):
    with ExitStack() as ctx:
        sems = []

        def sb(n, shape, dt):
            return ctx.enter_context(nc.sbuf_tensor(f"{name}_{n}", shape, dt))

        def ps(n, shape):
            return ctx.enter_context(nc.psum_tensor(f"{name}_{n}", shape, F32))

        def sem(n):
            sems.append(nc.alloc_semaphore(f"{name}_{n}"))
            return sems[-1]

        yield ctx, sb, ps, sem
    nc.clear_and_free_semaphores(sems)
    nc.all_engine_barrier()


def split_weights(nc, sem, name, jobs):
    PIECE = 2048
    pieces = []
    for src, hi, lo in jobs:
        for c in range(0, src.shape[1], PIECE):
            e = min(c + PIECE, src.shape[1])
            pieces.append((src[:, c:e], hi[:, c:e], lo[:, c:e], e - c))
    with ExitStack() as inner:
        stage = inner.enter_context(nc.sbuf_tensor(f"{name}_stage", [P, 2, PIECE], F32))
        loaded = [sem(f"w_loaded{i}") for i in range(2)]
        hi_done, lo_done = sem("w_hi_done"), sem("w_lo_done")
        block = inner.enter_context(nc.Block())

        @block.sync
        def _(sp):
            for i, (src, _, _, w) in enumerate(pieces):
                if i >= 2:
                    sp.wait_ge(lo_done, i - 1)
                sp.dma_start(stage[:, i % 2, 0:w], src).then_inc(loaded[i % 2], 16)

        @block.scalar
        def _(act):
            for i, (_, hi, _, w) in enumerate(pieces):
                act.wait_ge(loaded[i % 2], 16 * (i // 2 + 1))
                act.activation(hi, stage[:, i % 2, 0:w], ACT.Copy).then_inc(hi_done, 1)

        @block.vector
        def _(dve):
            for i, (_, hi, lo, w) in enumerate(pieces):
                dve.wait_ge(loaded[i % 2], 16 * (i // 2 + 1))
                dve.wait_ge(hi_done, i + 1)
                dve.tensor_tensor(lo, stage[:, i % 2, 0:w], f32(hi), ALU.subtract).then_inc(lo_done, 1)


def rows(w, width):
    return [w[k * P:(k + 1) * P, 0:width] for k in range(w.shape[0] // P)]


def weight(nc, ctx, name, kt, width):
    hi = ctx.enter_context(nc.sbuf_tensor(f"{name}_hi", [P, kt, width], F32R))
    lo = ctx.enter_context(nc.sbuf_tensor(f"{name}_lo", [P, kt, width], F32R))
    return hi, lo


def weight_jobs(w, dram):
    return [(src, w[0][:, k, :], w[1][:, k, :]) for k, src in enumerate(rows(dram, dram.shape[1]))]


def project(nc, name, x, tokens, weights, outs, ln=None, places=None):
    RING = 4
    full, rest = divmod(tokens, NB)
    rest_pad = -(-rest // P) * P
    BLOCKS = full + (rest > 0)
    LOOPS = (full - 1) // 2

    def products(width):
        found = []
        for src, wname, kind, dst in outs:
            if kind == "heads":
                found += [(src, wname, kind, dst, t) for t in range(width // P)]
            else:
                found += [(src, wname, kind, dst, m) for m in range(weights[wname].shape[1] // P)]
        return found

    STORE = 16 * (P // outs[0][3].shape[3] if outs[0][2] == "items" else 1)
    R = len(products(NB))
    uses = [len(range(s, R, RING)) for s in range(RING)]

    if ln is None:
        XL, NDVE, XH, NACT = 1, 1, 1, 1
        XT_READ = XL
    else:
        XL, XC, SQL, RSTD, XN, Z, ZL = 1, 2, 3, 4, 5, 5 + KT, 6 + KT
        XH, SQ, SQH, STD, ZH = 1, 2, 3, 4, 5
        NDVE, NACT = ZL, ZH
        XT_READ = XC

    with phase(nc, name) as (ctx, sb, ps, sem):
        W = {n: weight(nc, ctx, f"{name}_{n}", KT, w.shape[1]) for n, w in weights.items()}
        split_weights(nc, sem, name, [j for n, w in weights.items() for j in weight_jobs(W[n], w)])

        xt = [sb(f"xt{i}", [P, KT, NB], F32) for i in range(2)]
        raw = [(sb(f"xh{i}", [P, KT, NB], F32R), sb(f"xl{i}", [P, KT, NB], F32R)) for i in range(2)]
        if ln is not None:
            xc, sq = sb("xc", [P, KT, NB], F32), sb("sq", [P, KT, NB], F32)
            sqh, sql = sb("sqh", [P, KT, NB], F32R), sb("sql", [P, KT, NB], F32R)
            normed = [(sb(f"zh{i}", [P, KT, NB], F32R), sb(f"zl{i}", [P, KT, NB], F32R)) for i in range(2)]
            std, rstd = sb("std", [P, NB], F32), sb("rstd", [P, NB], F32)
            gb = sb("gb", [P, 2, KT], F32)
            eps = sb("eps", [P, 1], F32)
            inv_d, inv_dr = sb("inv_d", [P, P], F32), sb("inv_dr", [P, P], F32R)
            mean, var = ps("mean", [P, NB]), ps("var", [P, NB])
        out = [sb(f"out{i}", [P, 1024], F32R) for i in range(RING)]
        prod = [ps(f"prod{i}", [P, NB]) for i in range(RING)]

        x_loaded = [sem(f"x_loaded{i}") for i in range(2)]
        const_loaded, consts_done = sem("const_loaded"), sem("consts_done")
        dve_steps, act_steps, stats_done = sem("dve_steps"), sem("act_steps"), sem("stats_done")
        prod_done = [sem(f"prod_done{i}") for i in range(RING)]
        hi_done = [sem(f"hi_done{i}") for i in range(RING)]
        lo_done = [sem(f"lo_done{i}") for i in range(RING)]
        stored = [sem(f"stored{i}") for i in range(RING)]

        def width(n):
            return (rest, rest_pad) if isinstance(n, int) and n == full else (NB, NB)

        def blocks(eng):
            with eng.Fori(0, LOOPS) as i:
                yield i * 2, 0, i, True, True
                yield i * 2 + 1, 1, i, True, True
            for n in range(2 * LOOPS, BLOCKS):
                yield n, n % 2, n // 2, n + 1 < BLOCKS, n + 2 < BLOCKS

        def slot(n, i):
            return i % RING, n * uses[i % RING] + i // RING

        def halves(s, kind, dst, wp):
            if kind != "heads":
                return out[s][:, 0:wp], out[s][:, NB:NB + wp], prod[s][:, 0:wp]
            H, hd = dst.shape[0], dst.shape[3] // 2
            o = out[s][:, 0:H * 2 * hd].rearrange("p (h d) -> p h d", h=H)
            return o[:, :, 0:hd], o[:, :, hd:2 * hd], prod[s][:, 0:H * hd].rearrange("p (h d) -> p h d", h=H)

        def interleave(n, j, more, stages, do_product):
            todo = list(stages) if more else []
            made = products(width(n)[1])
            for i, p in enumerate(made):
                while todo and todo[0][0] * len(made) <= i:
                    todo.pop(0)[1](n + 1, 1 - j)
                do_product(n, j, i, *p)
            for _, f in todo:
                f(n + 1, 1 - j)

        block = ctx.enter_context(nc.Block())

        @block.sync
        def _(sp):
            if ln is not None:
                sp.dma_start(gb[:, 0, :], ln[0][:, :]).then_inc(const_loaded, 16)
                sp.dma_start(gb[:, 1, :], ln[1][:, :]).then_inc(const_loaded, 16)

            def load(n, j):
                w = width(n)[0]
                sp.dma_start(xt[j][:, :, 0:w],
                             x.rearrange("(k p) t -> p k t", p=P)[:, :, bass.ds(n * NB, w)]).then_inc(x_loaded[j], 16)

            def store(n, j, i, src, wn, kind, dst, m):
                s, before = slot(n, i)
                wp = width(n)[1]
                sp.wait_ge(lo_done[s], before + 1)
                if kind == "rows":
                    pairs = [(dst[:, m * P:(m + 1) * P, bass.ds(n * NB, wp)].rearrange("s p c -> p s c"), slice(0, P))]
                elif kind == "items":
                    hd = dst.shape[3]
                    pairs = [(dst[m * P // hd + g, bass.ds(n, 1)].rearrange("o s r c -> r (o s) c"),
                              slice(g * hd, (g + 1) * hd)) for g in range(P // hd)]
                else:
                    H, hd2 = dst.shape[0], dst.shape[3]
                    to = dst[:, :, bass.ds(n * (NB // P) + m, 1), :].rearrange("h p t d -> p h (t d)")
                    sp.dma_start(to, f32(out[s][:, 0:H * hd2]).rearrange("p (h d) -> p h d", h=H)).then_inc(stored[s], 16)
                    return
                of = f32(out[s][:, 0:2 * NB]).rearrange("p (s c) -> p s c", s=2)
                for to, at in pairs:
                    sp.dma_start(to, of[at, :, 0:wp]).then_inc(stored[s], 16)

            load(0, 0)
            load(1, 1)
            for n, j, _, more, two in blocks(sp):
                if two:
                    sp.wait_ge(dve_steps, n * NDVE + XT_READ)
                    load(n + 2, j)
                for i, p in enumerate(products(width(n)[1])):
                    store(n, j, i, *p)
            tail = len(products(rest_pad)) if rest else 0
            for s in range(RING):
                count = full * uses[s] + len(range(s, tail, RING))
                if count:
                    sp.wait_ge(stored[s], STORE * count)

        @block.scalar
        def _(act):
            def split(n, j):
                w = width(n)[0]
                act.wait_ge(x_loaded[j], (n + 2 - j) * 8)
                if not isinstance(n, int) or n > 1:
                    act.wait_ge(prod_done[(R - 1) % RING], (n - 1) * uses[(R - 1) % RING])
                act.activation(raw[j][0][:, :, 0:w], xt[j][:, :, 0:w], ACT.Copy).then_inc(act_steps, 1)

            def squares(n, j):
                w = width(n)[0]
                act.wait_ge(dve_steps, n * NDVE + XC)
                act.activation(sq[:, :, 0:w], xc[:, :, 0:w], ACT.Square).then_inc(act_steps, 1)
                act.wait_ge(act_steps, n * NACT + SQ)
                act.activation(sqh[:, :, 0:w], sq[:, :, 0:w], ACT.Copy).then_inc(act_steps, 1)

            def deviation(n, j):
                w = width(n)[0]
                act.wait_ge(stats_done, n * 2 + 2)
                act.activation(std[:, 0:w], var[:, 0:w], ACT.Sqrt, bias=eps[:, 0:1]).then_inc(act_steps, 1)

            def split_normed(n, j):
                w = width(n)[0]
                act.wait_ge(dve_steps, n * NDVE + Z)
                act.activation(normed[j][0][:, :, 0:w], xc[:, :, 0:w], ACT.Copy).then_inc(act_steps, 1)

            def evacuate(n, j, i, src, wn, kind, dst, m):
                s, before = slot(n, i)
                hi, _, y = halves(s, kind, dst, width(n)[1])
                act.wait_ge(prod_done[s], before + 1)
                act.wait_ge(stored[s], before * STORE)
                act.activation(hi, y, ACT.Copy).then_inc(hi_done[s], 1)

            stages = [(0, split)]
            if ln is not None:
                act.wait_ge(consts_done, 3)
                stages += list(zip(places["act"], (squares, deviation, split_normed)))
            for _, f in stages:
                f(0, 0)
            for n, j, _, more, _ in blocks(act):
                interleave(n, j, more, stages, evacuate)

        @block.vector
        def _(dve):
            def step(n, k, ins, wait=True):
                ins.then_inc(dve_steps, 1)
                if wait:
                    dve.wait_ge(dve_steps, n * NDVE + k)

            def split(n, j):
                w, wp = width(n)
                if wp > w:
                    dve.wait_ge(prod_done[(R - 1) % RING], (n - 1) * uses[(R - 1) % RING])
                    for t in raw[j] + (normed[j] if ln is not None else ()):
                        dve.memset(f32(t[:, :, w:wp]), 0.0)
                dve.wait_ge(act_steps, n * NACT + XH)
                step(n, XL, dve.tensor_tensor(raw[j][1][:, :, 0:w], xt[j][:, :, 0:w], f32(raw[j][0][:, :, 0:w]),
                                              ALU.subtract), False)

            def centre(n, j):
                w = width(n)[0]
                dve.wait_ge(stats_done, n * 2 + 1)
                step(n, XC, dve.tensor_tensor(xc[:, :, 0:w], xt[j][:, :, 0:w],
                                              mean[:, 0:w].unsqueeze(1).to_broadcast([P, KT, w]), ALU.subtract), False)

            def split_squares(n, j):
                w = width(n)[0]
                dve.wait_ge(act_steps, n * NACT + SQH)
                step(n, SQL, dve.tensor_tensor(sql[:, :, 0:w], sq[:, :, 0:w], f32(sqh[:, :, 0:w]), ALU.subtract), False)

            def norm(n, j):
                w = width(n)[0]
                dve.wait_ge(act_steps, n * NACT + STD)
                step(n, RSTD, dve.reciprocal(rstd[:, 0:w], std[:, 0:w]))
                step(n, XN, dve.tensor_tensor(sq[:, :, 0:w], xc[:, :, 0:w],
                                              rstd[:, 0:w].unsqueeze(1).to_broadcast([P, KT, w]), ALU.mult))
                for k in range(KT):
                    step(n, XN + k + 1, dve.tensor_scalar(xc[:, k, 0:w], sq[:, k, 0:w], gb[:, 0, k:k + 1],
                                                          gb[:, 1, k:k + 1], ALU.mult, ALU.add), False)

            def split_normed(n, j):
                w = width(n)[0]
                dve.wait_ge(act_steps, n * NACT + ZH)
                step(n, ZL, dve.tensor_tensor(normed[j][1][:, :, 0:w], xc[:, :, 0:w], f32(normed[j][0][:, :, 0:w]),
                                              ALU.subtract), False)

            def evacuate(n, j, i, src, wn, kind, dst, m):
                s, before = slot(n, i)
                hi, lo, y = halves(s, kind, dst, width(n)[1])
                dve.wait_ge(hi_done[s], before + 1)
                dve.tensor_tensor(lo, y, f32(hi), ALU.subtract).then_inc(lo_done[s], 1)

            stages = [(0, split)]
            if ln is not None:
                dve.memset(eps[:], LN_EPS).then_inc(consts_done, 1)
                dve.memset(inv_d[:], 1.0 / D).then_inc(consts_done, 1)
                dve.wait_ge(consts_done, 2)
                dve.tensor_copy(inv_dr[:], inv_d[:]).then_inc(consts_done, 1)
                dve.wait_ge(const_loaded, 32)
                stages += list(zip(places["dve"], (centre, split_squares, norm, split_normed)))
            for _, f in stages:
                f(0, 0)
            for n, j, _, more, _ in blocks(dve):
                interleave(n, j, more, stages, evacuate)

        @block.tensor
        def _(pe):
            def statistic(stat, parts, n, w):
                for i in range(2 * KT):
                    mm = pe.matmul(stat[:, 0:w], inv_dr[:], parts[i // KT][:, i % KT, 0:w],
                                   start=(i == 0), stop=(i == 2 * KT - 1))
                mm.then_inc(stats_done, 1)

            def find_mean(n, j):
                pe.wait_ge(dve_steps, n * NDVE + XL)
                statistic(mean, raw[j], n, width(n)[0])

            def find_variance(n, j):
                pe.wait_ge(dve_steps, n * NDVE + SQL)
                statistic(var, (sqh, sql), n, width(n)[0])

            def product(n, j, i, src, wn, kind, dst, m):
                s, before = slot(n, i)
                wp = width(n)[1]
                if i == 0:
                    pe.wait_ge(dve_steps, n * NDVE + NDVE)
                pe.wait_ge(lo_done[s], before)
                xs, ws = (raw if src == "raw" else normed)[j], W[wn]
                terms = [(k, a, b) for k in range(KT) for a, b in ((0, 0), (0, 1), (1, 0))]
                for t, (k, a, b) in enumerate(terms):
                    if kind == "heads":
                        c = ws[a].shape[2]
                        o, l, r = prod[s][:, 0:c], xs[b][:, k, m * P:(m + 1) * P], ws[a][:, k, :]
                    else:
                        o, l, r = prod[s][:, 0:wp], ws[a][:, k, m * P:(m + 1) * P], xs[b][:, k, 0:wp]
                    mm = pe.matmul(o, l, r, start=(t == 0), stop=(t == len(terms) - 1))
                mm.then_inc(prod_done[s], 1)

            stages = []
            if ln is not None:
                pe.wait_ge(consts_done, 3)
                stages = list(zip(places["pe"], (find_mean, find_variance)))
            for _, f in stages:
                f(0, 0)
            for n, j, _, more, _ in blocks(pe):
                interleave(n, j, more, stages, product)



GROUPS = ST // 2
RINGS = [0, 1, 2, 3, 4, 5] * (GROUPS // 6) + [6]
LAST_RING = RINGS[-1]
NRING = LAST_RING + 1
LAG = 4
SCORES = [([0, 1, 2] * ST)[:ST], ([0, 2, 1] * ST)[:ST]]
CHUNKS = 4
CHUNK = -(-S // (2 * CHUNKS)) * 2
UNITS = (NB // P) * CHUNKS
UNITS_AT = {0: [0, 1], 1: [2], 2: [3, 4], 3: [5], 4: [6, 7], 5: [8], 6: [9, 10], 7: [11], 8: [12, 13],
            9: [14, 15]}
ROW_AT = 11
POOL_LO = (1, 3, 5, 7, 9, 11)
DVE_HI = (9, 10, 11)
QB = T // NB


class Item:

    def __init__(self, pair, k, qb, j, half, prev_k=None, next_k=None, first=False, last=False, final_head=False,
                 last_two=False):
        self.final_head, self.last_two = final_head, last_two
        self.pair, self.k, self.qb, self.j = pair, k, qb, j
        self.h = pair * 2 + k
        self.n = self.h * QB + qb
        self.use = self.h * (QB // 2) + half
        self.prev_use = self.use if j == 1 else self.use - 1
        self.next_use = self.use if j == 0 else self.use + 1
        self.prev_k = k if prev_k is None else prev_k
        self.next_k = k if next_k is None else next_k
        self.starts_head, self.ends_head = prev_k is not None, next_k is not None
        self.first, self.last = first, last


def attention(nc, name, H, hd, q, k, v, acc_out, sums_out):
    SCALE = float(hd) ** -0.5
    ROW = 96
    C = ROW + 1
    M = 96
    PAIRS = H // 2
    LAST_KEYS = S - (ST - 1) * P

    with phase(nc, name) as (ctx, sb, ps, sem):

        kt = [sb(f"k{i}", [C, SPAD], F32R) for i in range(2)]
        vt = [sb(f"v{i}", [P, ST, M], F32R) for i in range(2)]
        qt = [sb(f"q{i}", [C, NB], F32R) for i in range(2)]
        qm = [sb(f"qm{i}", [ROW, NB], F32R) for i in range(2)]
        prob = [sb(f"prob{i}", [P, 2 * NB], F32) for i in range(NRING)]
        phi = [sb(f"phi{i}", [P, 2 * NB], F32R) for i in range(NRING)]
        plo = [sb(f"plo{i}", [P, 2 * NB], F32R) for i in range(NRING)]
        acc_sb = [sb(f"acc_sb{i}", [M, NB], F32) for i in range(2)]
        maxes = sb("maxes", [P, NB // P, CHUNKS], F32)
        negmax = sb("negmax", [P, NB // P], F32)
        ident = sb("ident", [P, P], F32)

        score = [ps(f"score{i}", [P, NB]) for i in range(3)]
        mscore = [ps(f"mscore{i}", [P, 2 * NB]) for i in range(2)]
        acc = ps("acc", [M, NB])

        k_loaded = [sem(f"k_loaded{i}") for i in range(2)]
        v_loaded = [sem(f"v_loaded{i}") for i in range(2)]
        q_loaded = [sem(f"q_loaded{i}") for i in range(2)]
        qm_loaded = [sem(f"qm_loaded{i}") for i in range(2)]
        filled, ident_done = sem("filled"), sem("ident_done")
        score_done = [sem(f"score_done{i}") for i in range(3)]
        exp_done = [sem(f"exp_done{i}") for i in range(NRING)]
        hi_done = [sem(f"hi_done{i}") for i in range(NRING)]
        lo_done = [sem(f"lo_done{i}") for i in range(NRING)]
        pv_done = [sem(f"pv_done{i}") for i in range(NRING)]
        unit_done, unit_read = sem("unit_done"), sem("unit_read")
        neg_done, row_done, row_copied = sem("neg_done"), sem("row_done"), sem("row_copied")
        acc_copied = sem("acc_copied")
        acc_stored = [sem(f"acc_stored{i}") for i in range(2)]

        def items(eng):
            def pair(p, first, last):
                for kk in range(2):
                    final = last and kk == 1
                    yield Item(p, kk, 0, 0, 0, prev_k=1 - kk, first=first and kk == 0, final_head=final)
                    with eng.Fori(0, QB // 2 - 1 - final) as i:
                        yield Item(p, kk, i * 2 + 1, 1, i)
                        yield Item(p, kk, i * 2 + 2, 0, i + 1)
                    if final:
                        yield Item(p, kk, QB - 3, 1, QB // 2 - 2)
                        yield Item(p, kk, QB - 2, 0, QB // 2 - 1, last_two=True)
                    yield Item(p, kk, QB - 1, 1, QB // 2 - 1, next_k=1 - kk, last=final, last_two=final)

            yield from pair(0, True, False)
            with eng.Fori(1, PAIRS - 1) as p:
                yield from pair(p, False, False)
            yield from pair(PAIRS - 1, False, True)

        def steps(it):
            return range(GROUPS + LAG) if it.last else range(GROUPS)

        def ring_uses(it, g):
            return it.n * RINGS.count(RINGS[g]) + RINGS[:g].count(RINGS[g])

        def score_buffer(j, use, t):
            b = SCORES[j][t]
            both = SCORES[0].count(b) + SCORES[1].count(b)
            return b, use * both + j * SCORES[0].count(b) + SCORES[j][:t].count(b)

        def score_read(it, t):
            b = SCORES[it.j][t]
            same = [u for u in range(t) if SCORES[it.j][u] == b]
            if same:
                g, odd = divmod(same[-1], 2)
                return RINGS[g], ring_uses(it, g) * 2 + odd + 1
            if it.first:
                return None
            g, odd = divmod(max(u for u in range(ST) if SCORES[1 - it.j][u] == b), 2)
            r = RINGS[g]
            return r, (it.n * RINGS.count(r) - RINGS[g:].count(r)) * 2 + odd + 1

        def lagged(it, s, lag):
            g = s - lag
            if g >= GROUPS or (g < 0 and it.first):
                return None
            if g >= 0:
                return g, RINGS[g], ring_uses(it, g), it.k
            g += GROUPS
            r = RINGS[g]
            return g, r, it.n * RINGS.count(r) - RINGS[g:].count(r), it.prev_k

        FILLS, REFILLS = [], []
        for i in range(2):
            FILLS.append((f32(vt[i][:]), 1.0))
            REFILLS.append((f32(vt[i][:, ST - 1, 2 * hd:M]), 0.0))
            FILLS += [(f32(kt[i][ROW:C, 0:S]), 1.0), (f32(kt[i][ROW:C, S:SPAD]), 0.0)]
            for at in range(3 * hd // 32 * 32, ROW, 32):
                FILLS += [(f32(x[i][at:at + 32, :]), 0.0) for x in (kt, qt, qm)]
        TOP = [(f32(vt[i][0:LAST_KEYS, ST - 1, 2 * hd:M]), 1.0) for i in range(2)]
        NFILL = len(FILLS) + len(REFILLS) + len(TOP)

        q_items = q.rearrange("h b s r c -> (h b) s r c")
        block = ctx.enter_context(nc.Block())

        @block.sync
        def _(sp):
            def load_kv(h, kk):
                rows = bass.ds(h * hd, hd)
                for at, half in ((0, 0), (hd, 1), (2 * hd, 0)):
                    sp.dma_start(f32(kt[kk][at:at + hd, :]), k[half, rows, :]).then_inc(k_loaded[kk], 16)
                sp.dma_start(f32(vt[kk][:, :, 0:2 * hd]),
                             v[bass.ds(h, 1)].rearrange("o p t d -> p (o t) d")).then_inc(v_loaded[kk], 16)

            def load_q(tile, n, loaded):
                for at, half in ((0, 0), (hd, 0), (2 * hd, 1)):
                    sp.dma_start(f32(tile[at:at + hd, :]),
                                 q_items[bass.ds(n, 1), half].rearrange("o r c -> (o r) c")).then_inc(loaded, 16)

            def store(h, qb, j, n):
                sp.wait_ge(acc_copied, n + 1)
                cols = bass.ds(qb * NB, NB)
                for i in range(2):
                    sp.dma_start(acc_out[i, bass.ds(h * hd, hd), cols],
                                 acc_sb[j][i * hd:(i + 1) * hd, :]).then_inc(acc_stored[j], 16)
                sp.dma_start(sums_out[bass.ds(h, 1), cols], acc_sb[j][2 * hd:2 * hd + 1, :]).then_inc(acc_stored[j], 16)

            sp.wait_ge(filled, NFILL)
            load_kv(0, 0)
            load_q(qm[0], 0, qm_loaded[0])
            load_q(qm[1], 1, qm_loaded[1])
            load_q(qt[0], 0, q_loaded[0])
            load_kv(1, 1)
            for it in items(sp):
                if not it.last:
                    if not it.first:
                        b, before = score_buffer(1 - it.j, it.prev_use, ST - 1)
                        sp.wait_ge(score_done[b], before + 1)
                    load_q(qt[1 - it.j], it.n + 1, q_loaded[1 - it.j])
                if not it.last_two:
                    sp.wait_ge(neg_done, it.n + 1)
                    load_q(qm[it.j], it.n + 2, qm_loaded[it.j])
                if not it.first:
                    if it.starts_head:
                        store(it.h - 1, QB - 1, 1 - it.j, it.n - 1)
                    else:
                        store(it.h, it.qb - 1, 1 - it.j, it.n - 1)
                if it.starts_head and not it.first and not it.final_head:
                    sp.wait_ge(pv_done[LAST_RING], it.h * QB)
                    load_kv(it.h + 1, 1 - it.k)
                if it.last:
                    store(it.h, it.qb, it.j, it.n)
            for j in range(2):
                sp.wait_ge(acc_stored[j], H * (QB // 2) * 48)

        @block.gpsimd
        def _(pool):
            pool.memset(ident[:], 0.0).then_inc(ident_done, 1)
            pool.wait_ge(ident_done, 1)
            pool.affine_select(out=ident[:], in_=ident[:], compare_op=ALU.not_equal, fill=1.0, base=0,
                               pattern=[[-1, P]], channel_multiplier=1).then_inc(ident_done, 1)
            for it in items(pool):
                for s in steps(it):
                    if (x := lagged(it, s, 2)) and x[0] in POOL_LO:
                        _, r, uses, _ = x
                        pool.wait_ge(hi_done[r], uses + 1)
                        pool.tensor_tensor(plo[r][:], prob[r][:], f32(phi[r][:]), ALU.subtract).then_inc(lo_done[r], 1)

        @block.scalar
        def _(act):
            def copy_row(j, n):
                act.wait_ge(row_done, n + 1)
                act.activation(qt[j][ROW:C, :], mscore[0][0:1, 0:NB], ACT.Copy).then_inc(row_copied, 1)

            def copy_acc(n, j, use):
                act.wait_ge(pv_done[LAST_RING], n + 1)
                act.wait_ge(acc_stored[j], use * 48)
                act.activation(acc_sb[j][0:2 * hd + 1, :], acc[0:2 * hd + 1, :], ACT.Copy).then_inc(acc_copied, 1)

            def exp(it, t):
                r = RINGS[t // 2]
                b, before = score_buffer(it.j, it.use, t)
                act.wait_ge(score_done[b], before + 1)
                act.activation(prob[r][:, t % 2 * NB:(t % 2 + 1) * NB], score[b][:], ACT.Exp,
                               scale=SCALE).then_inc(exp_done[r], 1)

            copy_row(0, 0)
            for it in items(act):
                for s in steps(it):
                    if s < GROUPS:
                        r = RINGS[s]
                        act.wait_ge(pv_done[r], ring_uses(it, s))
                        exp(it, 2 * s)
                    if (x := lagged(it, s, 1)) and x[0] not in DVE_HI:
                        _, r, uses, _ = x
                        act.wait_ge(exp_done[r], uses * 2 + 2)
                        act.activation(phi[r][:], prob[r][:], ACT.Copy).then_inc(hi_done[r], 1)
                    if s < GROUPS:
                        exp(it, 2 * s + 1)
                    if s == ROW_AT and not it.last:
                        copy_row(1 - it.j, it.n + 1)
                    if s == LAG - 1 and not it.first:
                        copy_acc(it.n - 1, 1 - it.j, it.prev_use)
                    if s == GROUPS + LAG - 1:
                        copy_acc(it.n, it.j, it.use)

        @block.vector
        def _(dve):
            def maximum(n, u):
                t, c = divmod(u, CHUNKS)
                w = min(CHUNK, S - c * CHUNK)
                dve.wait_ge(unit_done, n * UNITS + u + 1)
                dve.tensor_reduce(maxes[:, t, c:c + 1], mscore[u % 2][:, 0:w], AX.X, ALU.max).then_inc(unit_read, 1)
                if u == UNITS - 1:
                    dve.wait_ge(unit_read, n * UNITS + UNITS)
                    dve.tensor_reduce(negmax[:], maxes[:], AX.X, ALU.max, negate=True).then_inc(neg_done, 1)

            for ap, value in FILLS:
                dve.memset(ap, value).then_inc(filled, 1)
            dve.wait_ge(filled, len(FILLS))
            for ap, value in REFILLS:
                dve.memset(ap, value).then_inc(filled, 1)
            dve.wait_ge(filled, len(FILLS) + len(REFILLS))
            for ap, value in TOP:
                dve.memset(ap, value).then_inc(filled, 1)
            for u in range(UNITS):
                maximum(0, u)
            for it in items(dve):
                for s in steps(it):
                    if not it.last:
                        for u in UNITS_AT.get(s, ()):
                            maximum(it.n + 1, u)
                    if (x := lagged(it, s, 1)) and x[0] in DVE_HI:
                        _, r, uses, _ = x
                        dve.wait_ge(exp_done[r], uses * 2 + 2)
                        dve.tensor_copy(phi[r][:], prob[r][:]).then_inc(hi_done[r], 1)
                    if (x := lagged(it, s, 2)) and x[0] not in POOL_LO:
                        _, r, uses, _ = x
                        dve.wait_ge(hi_done[r], uses + 1)
                        dve.tensor_tensor(plo[r][:], prob[r][:], f32(phi[r][:]), ALU.subtract).then_inc(lo_done[r], 1)

        @block.tensor
        def _(pe):
            def unit(n, j, kk, u):
                t, c = divmod(u, CHUNKS)
                lo, hi = c * CHUNK, min((c + 1) * CHUNK, S)
                if not (isinstance(n, int) and n == 0 and u < 2):
                    pe.wait_ge(unit_read, n * UNITS + u - 1)
                for at in range(lo, hi, NB):
                    e = min(at + NB, hi)
                    mm = pe.matmul(mscore[u % 2][:, at - lo:e - lo], qm[j][:, t * P:(t + 1) * P],
                                   kt[kk][0:ROW, at:e], start=True, stop=True)
                mm.then_inc(unit_done, 1)

            def make_row(n):
                pe.wait_ge(neg_done, n + 1)
                for t in range(NB // P):
                    mm = pe.matmul(mscore[0][0:1, t * P:(t + 1) * P], negmax[:, t:t + 1], ident[:], start=True, stop=True)
                mm.then_inc(row_done, 1)

            pe.wait_ge(ident_done, 2)
            pe.wait_ge(k_loaded[0], 48)
            pe.wait_ge(qm_loaded[0], 48)
            for u in range(UNITS):
                unit(0, 0, 0, u)
            make_row(0)
            def scores(it, t):
                if x := score_read(it, t):
                    pe.wait_ge(exp_done[x[0]], x[1])
                b, _ = score_buffer(it.j, it.use, t)
                pe.matmul(score[b][:], kt[it.k][:, t * P:(t + 1) * P], qt[it.j][:],
                          start=True, stop=True).then_inc(score_done[b], 1)

            for it in items(pe):
                for s in steps(it):
                    if s == 0:
                        pe.wait_ge(q_loaded[it.j], (it.use + 1) * 48)
                        pe.wait_ge(row_copied, it.n + 1)
                    if s < GROUPS:
                        scores(it, 2 * s)
                    if not it.last:
                        if s == 0:
                            pe.wait_ge(qm_loaded[1 - it.j], (it.next_use + 1) * 48)
                            if it.ends_head:
                                pe.wait_ge(k_loaded[it.next_k], (it.pair + it.k + 1) * 48)
                        for u in UNITS_AT.get(s, ())[:1]:
                            unit(it.n + 1, 1 - it.j, it.next_k, u)
                        if s == ROW_AT:
                            make_row(it.n + 1)
                    if s < GROUPS:
                        scores(it, 2 * s + 1)
                    if not it.last:
                        for u in UNITS_AT.get(s, ())[1:]:
                            unit(it.n + 1, 1 - it.j, it.next_k, u)
                    if x := lagged(it, s, LAG):
                        g, r, uses, kk = x
                        if g == 0:
                            if it.starts_head:
                                pe.wait_ge(v_loaded[it.k], (it.pair + 1) * 16)
                            pe.wait_ge(acc_copied, it.n)
                        pe.wait_ge(hi_done[r], uses + 1)
                        pe.wait_ge(lo_done[r], uses + 1)
                        for i in range(2):
                            for part in (phi, plo):
                                t = 2 * g + i
                                mm = pe.matmul(acc[:], vt[kk][:, t, :], part[r][:, i * NB:(i + 1) * NB],
                                               start=(t == 0 and part is phi), stop=(t == ST - 1 and part is plo))
                        mm.then_inc(pv_done[r], 1)



def blocks_of(eng):
    B = T // NB
    with eng.Fori(0, B // 2 - 1) as i:
        yield i * 2, 0, i, True, True
        yield i * 2 + 1, 1, i, True, True
    yield B - 2, 0, B // 2 - 1, True, False
    yield B - 1, 1, B // 2 - 1, False, False


TERMS = ((0, 0), (0, 1), (1, 0))


def feature_tiles(ap, n):
    return ap.rearrange("(k p) t -> p k t", p=P)[:, :, bass.ds(n * NB, NB)]


def output_projection(nc, name, acc, sums, recips, x, wo, bo, out):
    KO = wo.shape[0] // P
    H = sums.shape[0]
    hd = wo.shape[0] // H
    HT = P // hd
    LOAD = 16 * (2 + H)
    spread = [t.rearrange("h (c t) -> (h c) t", c=P // H) for t in (sums, recips)]

    with phase(nc, name) as (ctx, sb, ps, sem):
        WO = weight(nc, ctx, f"{name}_wo", KO, D)
        split_weights(nc, sem, name, weight_jobs(WO, wo))

        biaso = sb("biaso", [P, KT], F32)
        part = [sb(f"part{i}", [P, 3, KO, NB], F32) for i in range(2)]
        total = sb("total", [P, H * T // P], F32)
        oh = [sb(f"oh{i}", [P, KO, NB], F32R) for i in range(2)]
        ol = [sb(f"ol{i}", [P, KO, NB], F32R) for i in range(2)]
        xin = [sb(f"xin{i}", [P, KT, NB], F32) for i in range(2)]
        xout = [sb(f"xout{i}", [P, KT, NB], F32) for i in range(2)]
        prod = [[ps(f"prod{i}{m}", [P, NB]) for m in range(KT)] for i in range(2)]

        const_loaded, sums_loaded = sem("const_loaded"), sem("sums_loaded")
        recip_done, recips_stored = sem("recip_done"), sem("recips_stored")
        acc_loaded = [sem(f"acc_loaded{i}") for i in range(2)]
        x_loaded = [sem(f"x_loaded{i}") for i in range(2)]
        stored = [sem(f"stored{i}") for i in range(2)]
        sum_done, o_done, hi_done, lo_done = sem("sum_done"), sem("o_done"), sem("hi_done"), sem("lo_done")
        prod_done, added = sem("prod_done"), [sem(f"added{i}") for i in range(2)]
        block = ctx.enter_context(nc.Block())

        @block.sync
        def _(sp):
            if bo is not None:
                sp.dma_start(biaso[:], bo[:, :]).then_inc(const_loaded, 16)

            def load_acc(n, j):
                for i in range(2):
                    sp.dma_start(part[j][:, i], feature_tiles(acc[i], n)).then_inc(acc_loaded[j], 16)

            def load_recips(n, j):
                for h in range(H):
                    at = h % HT * hd
                    sp.dma_start(part[j][at:at + hd, 2, h // HT, :],
                                 recips[h:h + 1, bass.ds(n * NB, NB)].broadcast_to([hd, NB])).then_inc(acc_loaded[j], 16)

            def load_x(n, j):
                sp.dma_start(xin[j][:], feature_tiles(x, n)).then_inc(x_loaded[j], 16)

            sp.dma_start(total[:], spread[0]).then_inc(sums_loaded, 16)
            for j in range(2):
                load_acc(j, j)
                load_x(j, j)
            sp.wait_ge(recip_done, 1)
            sp.dma_start(spread[1], total[:]).then_inc(recips_stored, 16)
            sp.wait_ge(recips_stored, 16)
            for j in range(2):
                load_recips(j, j)
            for n, j, i, more, two in blocks_of(sp):
                if two:
                    sp.wait_ge(lo_done, n + 1)
                    load_acc(n + 2, j)
                    load_recips(n + 2, j)
                sp.wait_ge(added[j], (i + 1) * KT)
                if two:
                    load_x(n + 2, j)
                sp.dma_start(feature_tiles(out, n), xout[j][:]).then_inc(stored[j], 16)
            for j in range(2):
                sp.wait_ge(stored[j], T // NB // 2 * 16)

        @block.vector
        def _(dve):
            def normalise(n, j, i):
                dve.wait_ge(acc_loaded[j], i * LOAD + LOAD)
                dve.tensor_tensor(part[j][:, 0], part[j][:, 0], part[j][:, 1], ALU.add).then_inc(sum_done, 1)
                dve.wait_ge(sum_done, n + 1)
                dve.tensor_tensor(part[j][:, 0], part[j][:, 0], part[j][:, 2], ALU.mult).then_inc(o_done, 1)

            def split(n, j):
                dve.wait_ge(hi_done, n + 1)
                dve.tensor_tensor(ol[j][:], part[j][:, 0], f32(oh[j][:]), ALU.subtract).then_inc(lo_done, 1)

            def add(n, j, i):
                dve.wait_ge(prod_done, n + 1)
                dve.wait_ge(x_loaded[j], i * 16 + 16)
                dve.wait_ge(stored[j], i * 16)
                for m in range(KT):
                    if bo is not None:
                        dve.scalar_tensor_tensor(xout[j][:, m], prod[j][m][:], biaso[:, m:m + 1], xin[j][:, m],
                                                 ALU.add, ALU.add).then_inc(added[j], 1)
                    else:
                        dve.tensor_tensor(xout[j][:, m], prod[j][m][:], xin[j][:, m], ALU.add).then_inc(added[j], 1)

            if bo is not None:
                dve.wait_ge(const_loaded, 16)
            dve.wait_ge(sums_loaded, 16)
            dve.reciprocal(total[:], total[:]).then_inc(recip_done, 1)
            normalise(0, 0, 0)
            split(0, 0)
            for n, j, i, more, _ in blocks_of(dve):
                if more:
                    normalise(n + 1, 1 - j, i + j)
                    split(n + 1, 1 - j)
                add(n, j, i)

        @block.scalar
        def _(act):
            def split(n, j):
                act.wait_ge(o_done, n + 1)
                act.activation(oh[j][:], part[j][:, 0], ACT.Copy).then_inc(hi_done, 1)

            split(0, 0)
            for n, j, _, more, _ in blocks_of(act):
                if more:
                    act.wait_ge(prod_done, n)
                    split(n + 1, 1 - j)

        @block.tensor
        def _(pe):
            for n, j, i, _, _ in blocks_of(pe):
                pe.wait_ge(lo_done, n + 1)
                pe.wait_ge(added[j], i * KT)
                for d in range(KT):
                    for t, (k, a, c) in enumerate([(k, a, c) for k in range(KO) for a, c in TERMS]):
                        mm = pe.matmul(prod[j][d][:], WO[a][:, k, d * P:(d + 1) * P], (oh, ol)[c][j][:, k],
                                       start=(t == 0), stop=(t == 3 * KO - 1))
                mm.then_inc(prod_done, 1)


def feed_forward(nc, name, x, w1, b1, func, w2, b2, out):
    F = w1.shape[1]
    FT = F // P
    HALF = FT // 2

    with phase(nc, name) as (ctx, sb, ps, sem):
        W1, W2 = weight(nc, ctx, f"{name}_w1", KT, F), weight(nc, ctx, f"{name}_w2", FT, D)
        split_weights(nc, sem, name, weight_jobs(W1, w1) + weight_jobs(W2, w2))

        bias1, bias2 = sb("bias1", [P, FT], F32), sb("bias2", [P, KT], F32)
        X = [sb(f"X{i}", [P, KT, NB], F32) for i in range(2)]
        xh = [sb(f"xh{i}", [P, KT, NB], F32R) for i in range(2)]
        xl = [sb(f"xl{i}", [P, KT, NB], F32R) for i in range(2)]
        y = sb("y", [P, KT, NB], F32)
        h = [sb(f"h{i}", [P, NB], F32) for i in range(2)]
        hh = [sb(f"hh{i}", [P, NB], F32R) for i in range(2)]
        hl = [sb(f"hl{i}", [P, NB], F32R) for i in range(2)]
        hp = [ps(f"hp{i}", [P, NB]) for i in range(2)]
        yp = [ps(f"yp{m}", [P, NB]) for m in range(KT)]

        const_loaded = sem("const_loaded")
        x_loaded = [sem(f"x_loaded{i}") for i in range(2)]
        xh_done, xl_done = sem("xh_done"), sem("xl_done")
        hp_done = [sem(f"hp_done{i}") for i in range(2)]
        h_done = [sem(f"h_done{i}") for i in range(2)]
        hh_done = [sem(f"hh_done{i}") for i in range(2)]
        hl_done = [sem(f"hl_done{i}") for i in range(2)]
        used = [sem(f"used{i}") for i in range(2)]
        y_done, stored = sem("y_done"), sem("stored")
        block = ctx.enter_context(nc.Block())

        def hidden(n, j, more):
            return [(n, j, m) for m in range(1, FT)] + ([(n + 1, 1 - j, 0)] if more else [])

        def uses(n, m):
            return m % 2, n * HALF + m // 2

        SPLIT_AT = {m: [] for m in range(1, FT)}
        for k in range(KT):
            SPLIT_AT[min(FT // 2 + k * (FT // 2) // KT, FT - 1)].append(k)

        @block.sync
        def _(sp):
            sp.dma_start(bias1[:], b1[:, :]).then_inc(const_loaded, 16)
            sp.dma_start(bias2[:], b2[:, :]).then_inc(const_loaded, 16)
            for j in range(2):
                sp.dma_start(X[j][:], feature_tiles(x, j)).then_inc(x_loaded[j], 16)
            for n, j, _, _, two in blocks_of(sp):
                sp.wait_ge(y_done, (n + 1) * KT)
                if two:
                    sp.dma_start(X[j][:], feature_tiles(x, n + 2)).then_inc(x_loaded[j], 16)
                sp.dma_start(feature_tiles(out, n), y[:]).then_inc(stored, 16)
            sp.wait_ge(stored, T // NB * 16)

        @block.scalar
        def _(act):
            def split(j, i, k):
                if k == 0:
                    act.wait_ge(x_loaded[j], i * 16 + 16)
                act.activation(xh[j][:, k], X[j][:, k], ACT.Copy).then_inc(xh_done, 1)

            def tile(n, m):
                b, before = uses(n, m)
                act.wait_ge(hp_done[b], before + 1)
                act.wait_ge(hl_done[b], before)
                act.activation(h[b][:], hp[b][:], func, bias=bias1[:, m:m + 1]).then_inc(h_done[b], 1)
                act.wait_ge(h_done[b], before + 1)
                act.wait_ge(used[b], before)
                act.activation(hh[b][:], h[b][:], ACT.Copy).then_inc(hh_done[b], 1)

            act.wait_ge(const_loaded, 32)
            for k in range(KT):
                split(0, 0, k)
            tile(0, 0)
            for n, j, i, more, _ in blocks_of(act):
                for nn, _, m in hidden(n, j, more):
                    for k in SPLIT_AT.get(m, ()) if more else ():
                        split(1 - j, i + j, k)
                    tile(nn, m)

        @block.vector
        def _(dve):
            def split(n, j, k):
                dve.wait_ge(xh_done, n * KT + k + 1)
                dve.tensor_tensor(xl[j][:, k], X[j][:, k], f32(xh[j][:, k]), ALU.subtract).then_inc(xl_done, 1)

            def tile(n, m):
                b, before = uses(n, m)
                dve.wait_ge(hh_done[b], before + 1)
                dve.tensor_tensor(hl[b][:], h[b][:], f32(hh[b][:]), ALU.subtract).then_inc(hl_done[b], 1)

            dve.wait_ge(const_loaded, 32)
            for k in range(KT):
                split(0, 0, k)
            tile(0, 0)
            for n, j, _, more, _ in blocks_of(dve):
                for nn, _, m in hidden(n, j, more):
                    for k in SPLIT_AT.get(m, ()) if more else ():
                        split(n + 1, 1 - j, k)
                    tile(nn, m)
                dve.wait_ge(used[(FT - 1) % 2], n * HALF + HALF)
                dve.wait_ge(stored, n * 16)
                for m in range(KT):
                    dve.scalar_tensor_tensor(y[:, m], yp[m][:], bias2[:, m:m + 1], X[j][:, m],
                                             ALU.add, ALU.add).then_inc(y_done, 1)

        @block.tensor
        def _(pe):
            def hidden_tile(n, j, m):
                b, before = uses(n, m)
                if m == 0:
                    pe.wait_ge(xl_done, (n + 1) * KT)
                pe.wait_ge(h_done[b], before)
                for t, (k, a, c) in enumerate([(k, a, c) for k in range(KT) for a, c in TERMS]):
                    mm = pe.matmul(hp[b][:], W1[a][:, k, m * P:(m + 1) * P], (xh, xl)[c][j][:, k],
                                   start=(t == 0), stop=(t == 3 * KT - 1))
                mm.then_inc(hp_done[b], 1)

            def use_hidden(n, m):
                b, before = uses(n, m)
                pe.wait_ge(hl_done[b], before + 1)
                if m == 0:
                    pe.wait_ge(y_done, n * KT)
                for a, c in TERMS:
                    for d in range(KT):
                        mm = pe.matmul(yp[d][:], W2[a][:, m, d * P:(d + 1) * P], (hh, hl)[c][b][:],
                                       start=(m == 0 and (a, c) == (0, 0)), stop=(m == FT - 1 and (a, c) == (1, 0)))
                mm.then_inc(used[b], 1)

            hidden_tile(0, 0, 0)
            for n, j, _, more, _ in blocks_of(pe):
                for nn, jj, m in hidden(n, j, more):
                    hidden_tile(nn, jj, m)
                    use_hidden(n, m - 1 if m else FT - 1)
                if not more:
                    use_hidden(n, FT - 1)


def build(nc, a, out):
    L0, L1 = (8, 16), (16, 32)

    def scratch(n, shape):
        return nc.dram_tensor(n, shape, F32).ap()

    q, k, v, acc, sums, recips = [], [], [], [], [], []
    for i, (H, hd) in enumerate((L0, L1)):
        q.append(scratch(f"q{i}", [H, QB, 2, hd, NB]))
        k.append(scratch(f"k{i}", [2, H * hd, SPAD]))
        v.append(scratch(f"v{i}", [H, P, ST, 2 * hd]))
        acc.append(scratch(f"acc{i}", [2, H * hd, T]))
        sums.append(scratch(f"sums{i}", [H, T]))
        recips.append(scratch(f"recips{i}", [H, T]))
    x1, mid = scratch("x1", [D, T]), [scratch(f"mid{i}", [D, T]) for i in range(2)]
    ctx_t, x = a["ctx_1024"], a["x"]

    project(nc, "kv", ctx_t, S,
            {"k0": a["L0_xattn_W_k"], "v0": a["L0_xattn_W_v"], "k1": a["L1_xattn_Wkv"][:, 0:D], "v1": a["L1_xattn_Wkv"][:, D:2 * D]},
            [("raw", "k0", "rows", k[0]), ("raw", "v0", "heads", v[0]),
             ("ln", "k1", "rows", k[1]), ("ln", "v1", "heads", v[1])],
            ln=(a["L1_xattn_ln_kv_g"], a["L1_xattn_ln_kv_b"]),
            places={"pe": (0.15, 0.55), "dve": (0.2, 0.4, 0.6, 0.9), "act": (0.2, 0.6, 0.9)})
    project(nc, "pq0", x, T, {"q0": a["L0_xattn_W_q"]}, [("raw", "q0", "items", q[0])])
    attention(nc, "a0", *L0, q[0], k[0], v[0], acc[0], sums[0])
    output_projection(nc, "o0", acc[0], sums[0], recips[0], x, a["L0_xattn_W_o"], None, mid[0])
    feed_forward(nc, "f0", mid[0], a["L0_xattn_w1"], a["L0_xattn_b1"], ACT.Relu, a["L0_xattn_w2"], a["L0_xattn_b2"], x1)
    project(nc, "pq1", x1, T, {"q1": a["L1_xattn_Wq"]}, [("ln", "q1", "items", q[1])],
            ln=(a["L1_xattn_ln_q_g"], a["L1_xattn_ln_q_b"]),
            places={"pe": (0.25, 1), "dve": (0, 0.25, 0.5, 0.5), "act": (0.25, 0.25, 1)})
    attention(nc, "a1", *L1, q[1], k[1], v[1], acc[1], sums[1])
    output_projection(nc, "o1", acc[1], sums[1], recips[1], x1, a["L1_xattn_Wo"], a["L1_xattn_bo"], mid[1])
    feed_forward(nc, "f1", mid[1], a["L1_xattn_W1"], a["L1_xattn_b1"], ACT.Silu, a["L1_xattn_W2"], a["L1_xattn_b2"], out)


TRANSPOSED = {"x", "ctx_1024", "L0_xattn_w1", "L0_xattn_w2", "L1_xattn_Wq", "L1_xattn_Wkv", "L1_xattn_Wo",
              "L1_xattn_W1", "L1_xattn_W2"}


def kernel(**inputs):
    import numpy as np
    import concourse.bacc as bacc
    from concourse.bass_utils import run_bass_kernel_spmd

    nc = bacc.Bacc("TRN2", target_bir_lowering=False, num_devices=1)
    arrays, aps = {}, {}
    for name, value in inputs.items():
        a = np.asarray(value)
        if name in ("x", "ctx_1024"):
            a = a[0]
        if a.ndim == 1:
            a = a.reshape(-1, P)
        if name in TRANSPOSED or value.ndim == 1:
            a = a.T
        a = np.ascontiguousarray(a)
        arrays[f"in_{name}"] = a
        aps[name] = nc.dram_tensor(f"in_{name}", a.shape, mybir.dt.from_np(a.dtype), kind="ExternalInput").ap()
    out = nc.dram_tensor("out_t", (D, T), F32, kind="ExternalOutput").ap()
    build(nc, aps, out)
    r = run_bass_kernel_spmd(nc, [arrays], core_ids=[0])
    return np.ascontiguousarray(r.results[0]["out_t"].T)[None]
```
